# Optimizing a Trainium2 kernel written in Bass

```python
import numpy as np
import jax
import jax.numpy as jnp

def _softmax(x, axis=-1):
    return jax.nn.softmax(x, axis=axis)

def _gelu(x):
    return jax.nn.gelu(x, approximate=True)

def _silu(x):
    return jax.nn.silu(x)

def _sigmoid(x):
    return jax.nn.sigmoid(x)

def _layernorm(x, axis=-1, eps=1e-05):
    m = jnp.mean(x, axis=axis, keepdims=True)
    v = jnp.var(x, axis=axis, keepdims=True)
    return (x - m) / jnp.sqrt(v + eps)

def _scatter_add(tgt, idx, src, axis=0):
    return tgt.at[idx].add(src)

def _segment_sum(src, seg, n):
    return jax.ops.segment_sum(src, seg, n)
kernel_name = 'mk_seq_preln_d1_jaxref_r8_35d602'

def setup_inputs(seed: int=0):
    np.random.seed(seed)
    _w = jnp.asarray

    def _L0_attn_setup():
        import jax, jax.numpy as jnp
        import numpy as np
        import math
        B, L, D, H = (32, 64, 512, 32)
        HD = D // H
        key = jax.random.key(seed)
        ks = jax.random.split(key, 9)
        s = 1.0 / math.sqrt(D)
        return {'x': jax.random.normal(ks[0], (B, L, D), jnp.float32), 'Wq': jax.random.normal(ks[1], (D, D), jnp.float32) * s, 'bq': jax.random.normal(ks[2], (D,), jnp.float32) * s, 'Wk': jax.random.normal(ks[3], (D, D), jnp.float32) * s, 'bk': jax.random.normal(ks[4], (D,), jnp.float32) * s, 'Wv': jax.random.normal(ks[5], (D, D), jnp.float32) * s, 'bv': jax.random.normal(ks[6], (D,), jnp.float32) * s, 'Wo': jax.random.normal(ks[7], (D, D), jnp.float32) * s, 'bo': jax.random.normal(ks[8], (D,), jnp.float32) * s}
    _L0_attn_in = _L0_attn_setup()

    def _L0_ffn_setup():
        import jax, jax.numpy as jnp
        import numpy as np
        EPS = 1e-05

        def _bitlinear(x, w):
            scale = jnp.mean(jnp.abs(w))
            q = jnp.round(jnp.clip(w / (scale + EPS), -1.0, 1.0))
            deq = q * scale
            return x @ deq.T
        key = jax.random.key(seed)
        k1, k2, k3, k4 = jax.random.split(key, 4)
        B, S, H, I = (4, 256, 512, 1376)
        return {'hidden_states': jax.random.normal(k1, (B, S, H), dtype=jnp.float32), 'w_gate': jax.random.normal(k2, (I, H), dtype=jnp.float32) * 0.02, 'w_up': jax.random.normal(k3, (I, H), dtype=jnp.float32) * 0.02, 'w_down': jax.random.normal(k4, (H, I), dtype=jnp.float32) * 0.02}
    _L0_ffn_in = _L0_ffn_setup()
    _d = {'L0_attn_x': _L0_attn_in['x'], 'L0_attn_Wq': _L0_attn_in['Wq'], 'L0_attn_bq': _L0_attn_in['bq'], 'L0_attn_Wk': _L0_attn_in['Wk'], 'L0_attn_bk': _L0_attn_in['bk'], 'L0_attn_Wv': _L0_attn_in['Wv'], 'L0_attn_bv': _L0_attn_in['bv'], 'L0_attn_Wo': _L0_attn_in['Wo'], 'L0_attn_bo': _L0_attn_in['bo'], 'L0_ffn_w_gate': _L0_ffn_in['w_gate'], 'L0_ffn_w_up': _L0_ffn_in['w_up'], 'L0_ffn_w_down': _L0_ffn_in['w_down']}
    _x0 = _d['L0_attn_x']
    _d['L0_attn_x'] = jax.random.normal(jax.random.fold_in(jax.random.key(seed), 1), (4, 512, 512), dtype=_x0.dtype)
    del _x0
    return _d

def reference(L0_attn_x, L0_attn_Wq, L0_attn_bq, L0_attn_Wk, L0_attn_bk, L0_attn_Wv, L0_attn_bv, L0_attn_Wo, L0_attn_bo, L0_ffn_w_gate, L0_ffn_w_up, L0_ffn_w_down):

    def _L0_attn_ref(x, Wq, bq, Wk, bk, Wv, bv, Wo, bo):
        import jax, jax.numpy as jnp
        import numpy as np
        import math
        B, L, D, H = (32, 64, 512, 32)
        HD = D // H
        b, l, d = x.shape
        h, hd = (H, HD)
        q = (x @ Wq.T + bq).reshape(b, l, h, hd).transpose(0, 2, 1, 3)
        k = (x @ Wk.T + bk).reshape(b, l, h, hd).transpose(0, 2, 1, 3)
        v = (x @ Wv.T + bv).reshape(b, l, h, hd).transpose(0, 2, 1, 3)
        scores = jnp.einsum('bhqd,bhkd->bhqk', q, k) / math.sqrt(hd)
        causal = jnp.tril(jnp.ones((l, l), bool))
        scores = jnp.where(causal, scores, -jnp.inf)
        att = jax.nn.softmax(scores, axis=-1)
        out = jnp.einsum('bhqk,bhkd->bhqd', att, v)
        out = out.transpose(0, 2, 1, 3).reshape(b, l, d)
        return out @ Wo.T + bo

    def _L0_ffn_ref(hidden_states, w_gate, w_up, w_down):
        import jax, jax.numpy as jnp
        import numpy as np
        EPS = 1e-05

        def _bitlinear(x, w):
            scale = jnp.mean(jnp.abs(w))
            q = jnp.round(jnp.clip(w / (scale + EPS), -1.0, 1.0))
            deq = q * scale
            return x @ deq.T
        gate = _bitlinear(hidden_states, w_gate)
        up = _bitlinear(hidden_states, w_up)
        inter = gate * up
        out = _bitlinear(inter, w_down)
        return out
    x = L0_attn_x
    x = x + _L0_attn_ref(_layernorm(x, axis=-1), L0_attn_Wq, L0_attn_bq, L0_attn_Wk, L0_attn_bk, L0_attn_Wv, L0_attn_bv, L0_attn_Wo, L0_attn_bo)
    x = x + _L0_ffn_ref(_layernorm(x, axis=-1), L0_ffn_w_gate, L0_ffn_w_up, L0_ffn_w_down)
    return x

_drawn_inputs = setup_inputs


def setup_inputs(seed=0):
    import zlib

    import numpy as np

    out = dict(_drawn_inputs(seed))
    spreads = {}
    factors = {'L0_attn_bq': 8.0, 'L0_attn_bk': 8.0}
    for name, (base, spread) in spreads.items():
        noise = np.random.default_rng([zlib.crc32(name.encode()), seed]).standard_normal(out[name].shape)
        drawn = base * np.exp(spread * noise) if base else spread * noise
        out[name] = jnp.asarray(drawn.astype(out[name].dtype))
    for name, factor in factors.items():
        out[name] = (out[name] * factor).astype(out[name].dtype)
    return out
```

```python
import concourse.bass as bass
from concourse import mybir
from contextlib import ExitStack

F32 = mybir.dt.float32
F32R = mybir.dt.float32r
F16 = mybir.dt.float16
BF16 = mybir.dt.bfloat16
ALU = mybir.AluOpType
ACT = mybir.ActivationFunctionType
AX = mybir.AxisListType

P = 128
B, L, D = 4, 512, 512
H = 32
HD = D // H
I = 1376
NT = L // P
NC = D // P
NI = -(-I // P)
IR = I - (NI - 1) * P
BLOCKS = D // P
QH = 4
QUADS = H // QH
SLOTS = 3
EPS = 1e-5
X2_SCALE = 64.0
INTER_SCALE = 2.0 ** -15
OUT_SCALE = 1.0 / (X2_SCALE * X2_SCALE * INTER_SCALE)
NEG = -1e30
MROW = 96

SEG = {0: (0, 0), 1: (512, 128), 3: (896, 384), 2: (1024, 256)}
PW = 1280

UNITS = [("q", 0), ("k", 0)] + [("max", 0, p, u) for p in range(2) for u in range(3)] + [("m", 0)]
for _t in range(QUADS):
    if _t % 2 == 0 and _t // 2 + 1 < BLOCKS:
        UNITS += [("q", _t // 2 + 1), ("k", _t // 2 + 1)]
    if _t + 1 < QUADS:
        UNITS += [("max", _t + 1, p, u) for p in range(2) for u in range(3)] + [("m", _t + 1)]
UNIT = {u: n for n, u in enumerate(UNITS)}
PER_SLOT = len(UNITS) // 2
assert len(UNITS) % 2 == 0
FILLS = 3 * QH * QUADS


def preln_block(nc, x, wq, bq, wk, bk, wv, bv, wo, bo, wg, wu, wd, out):
    ctx = ExitStack()
    with ctx:
        def sb(name, shape, dt, where=ctx):
            return where.enter_context(nc.sbuf_tensor(name, shape, dt))

        def sem(name):
            return ctx.enter_context(nc.semaphore(name))

        wq_sb = sb("wq_sb", [P, NC, D], F32)
        wk_sb = sb("wk_sb", [P, NC, D], F32)
        wv_sb = sb("wv_sb", [P, NC, D], F32)
        wo_sb = sb("wo_sb", [P, NC, D], F32)
        tg = sb("tg", [P, NC, I], F16)
        tu = sb("tu", [P, NC, I], F16)
        td = sb("td", [P, NI, D], F16)
        bq_sb = sb("bq_sb", [P, BLOCKS], F32)
        bk_sb = sb("bk_sb", [P, BLOCKS], F32)
        bv_sb = sb("bv_sb", [P, D], F32)
        bo_sb = sb("bo_sb", [P, D], F32)
        ident = sb("ident", [P, P], F32)
        ident_b = sb("ident_b", [P, P], BF16)
        future = sb("future", [P, P], BF16)
        ones = sb("ones", [P, P], F32)
        is_even = sb("is_even", [P, 1], F32)
        is_odd = sb("is_odd", [P, 1], F32)
        minus_half = sb("minus_half", [P, NT], F32)
        absum = sb("absum", [P, 4], F32)
        wscale = sb("wscale", [P, 3], F32)
        wthr = sb("wthr", [P, 3], F32)
        wnthr = sb("wnthr", [P, 3], F32)
        fscale = sb("fscale", [P, 2], F32)
        x_sb = sb("x_sb", [P, NT, D], F32)
        stats = sb("stats", [P, NT, 6], F32)
        mv = sb("mv", [P, NT, 2], F32)
        rstd = sb("rstd", [P, NT, 1], F32)

        setup = ExitStack()
        wg_raw = sb("wg_raw", [P, NC, I], F32, setup)
        wu_raw = sb("wu_raw", [P, NC, I], F32, setup)
        wd_raw = sb("wd_raw", [P, NI, D], F32, setup)
        setup.close()

        v_aug = sb("v_aug", [P, NT, H // 2, 64], F32)
        qstk = [sb(f"qstk{s}", [P, QH, L], F32R) for s in range(SLOTS)]
        kstk = [sb(f"kstk{s}", [P, QH, L], F32R) for s in range(SLOTS)]
        attn = ExitStack()
        xT = sb("xT", [P, NC, L], F32, attn)
        qf = sb("qf", [P, L], F32, attn)
        kf = sb("kf", [P, L], F32, attn)
        qh = sb("qh", [P, L], F32R, attn)
        ql = sb("ql", [P, L], F32R, attn)
        kh = sb("kh", [P, L], F32R, attn)
        kl = sb("kl", [P, L], F32R, attn)
        mx = [sb(f"mx{s}", [P, NT, QH], F32, attn) for s in range(2)]
        mneg = [sb(f"mneg{s}", [QH, L], F32R, attn) for s in range(2)]
        aT = sb("aT", [P, BLOCKS, L], F32, attn)
        even_num = sb("even_num", [P, L], F32, attn)
        even_den = sb("even_den", [P, L], F32, attn)
        num = sb("num", [P, L], F32, attn)
        den_far = sb("den_far", [P, L], F32, attn)
        den = sb("den", [P, L], F32, attn)
        rden = sb("rden", [P, L], F32, attn)
        early = ExitStack()
        xn = sb("xn", [P, NT, D], F32, early)
        early.close()
        probs = sb("probs", [P, QH, PW], F32, attn)
        attn.close()

        ffn = ExitStack()
        xn2 = sb("xn2", [P, NT, D], F32, ffn)
        x2h = sb("x2h", [P, NC, L], F16, ffn)
        x2l = sb("x2l", [P, NC, L], F16, ffn)
        gate_s = [sb(f"gate_s{s}", [P, L], F32, ffn) for s in range(2)]
        inter = [sb(f"inter{s}", [P, L], F32, ffn) for s in range(2)]
        ih = sb("ih", [P, NI, L], F16, ffn)
        il = sb("il", [P, NI, L], F16, ffn)
        y_sb = sb("y_sb", [P, NT, D], F32, ffn)
        ffn.close()

        ps = ctx.enter_context(nc.psum_tensor("ps", [P, 8, 512], F32))

        x_loaded = sem("x_loaded")
        wqkv_loaded = sem("wqkv_loaded")
        wo_loaded = sem("wo_loaded")
        bias_loaded = sem("bias_loaded")
        ffnw_loaded = [sem(f"ffnw_loaded{n}") for n in range(3)]
        const_ready = sem("const_ready")
        abs_done = sem("abs_done")
        sums_ready = sem("sums_ready")
        thr_ready = sem("thr_ready")
        tern = sem("tern")
        setup_done = sem("setup_done")
        bq_ready = sem("bq_ready")
        mv_ready = sem("mv_ready")
        rstd_step = sem("rstd_step")
        rstd_ready = sem("rstd_ready")
        xn_ready = sem("xn_ready")
        xT_ps = sem("xT_ps")
        xT_act = sem("xT_act")
        xT_dve = sem("xT_dve")
        v_ps = sem("v_ps")
        v_ready = sem("v_ready")
        xbo_ready = sem("xbo_ready")
        unit_ready = sem("unit_ready")
        unit_free = [sem(f"unit_free{s}") for s in range(2)]
        qkf_ready = sem("qkf_ready")
        split_done = sem("split_done")
        split_step = sem("split_step")
        stack_ready = [sem(f"stack_ready{s}") for s in range(SLOTS)]
        max_ready = sem("max_ready")
        mneg_ready = sem("mneg_ready")
        mrow_ready = sem("mrow_ready")
        scores_ready = sem("scores_ready")
        exp_done = sem("exp_done")
        probs_masked = sem("probs_masked")
        pv_done = sem("pv_done")
        even_parts = sem("even_parts")
        norm_dve = sem("norm_dve")
        den_step = sem("den_step")
        den_moved = sem("den_moved")
        aT_ready = sem("aT_ready")
        pool_alone = sem("pool_alone")
        dve_alone = sem("dve_alone")
        sp_alone = sem("sp_alone")
        wo_ps = sem("wo_ps")
        x1_ready = sem("x1_ready")
        x2h_ready = sem("x2h_ready")
        x2l_ready = sem("x2l_ready")
        gu_ps = sem("gu_ps")
        gate_ready = sem("gate_ready")
        inter_ready = sem("inter_ready")
        ih_ready = sem("ih_ready")
        il_ready = sem("il_ready")
        down_ps = sem("down_ps")
        y_ready = sem("y_ready")
        stored = sem("stored")

        x_v = x.rearrange("b (t p) d -> b p t d", p=P)
        out_v = out.rearrange("b (t p) d -> b p t d", p=P)
        block = ctx.enter_context(nc.Block())

        @block.sync
        def _(sp):
            for dst, src in ((wq_sb, wq), (wk_sb, wk), (wv_sb, wv)):
                sp.dma_start(dst[:], src.rearrange("(c p) n -> p c n", p=P)).then_inc(wqkv_loaded, 16)
            sp.dma_start(wg_raw[:], wg.rearrange("(c p) n -> p c n", p=P)).then_inc(ffnw_loaded[0], 16)
            sp.dma_start(wu_raw[:], wu.rearrange("(c p) n -> p c n", p=P)).then_inc(ffnw_loaded[1], 16)
            sp.dma_start(wd_raw[:, 0:NI - 1, :], wd[0:(NI - 1) * P, :].rearrange("(c p) n -> p c n", p=P)).then_inc(ffnw_loaded[2], 16)
            sp.dma_start(wd_raw[0:IR, NI - 1, :], wd[(NI - 1) * P:I, :]).then_inc(ffnw_loaded[2], 16)
            sp.dma_start(wo_sb[:], wo.rearrange("(c p) n -> p c n", p=P)).then_inc(wo_loaded, 16)

            def stack(b, t):
                s, blk, e = t % SLOTS, t // 2, t % 2
                sp.wait_ge(split_done, b * 4 * BLOCKS + 4 * blk + 4)
                if t >= SLOTS:
                    sp.sem_inc(sp_alone, 1)
                    sp.wait_ge(scores_ready, b * FILLS + 3 * QH * (t - SLOTS + 1))
                for n, (qs, ks) in enumerate(((qh, kh), (ql, kh), (qh, kl), (ql, kl))):
                    for stk, part in ((qstk, qs), (kstk, ks)):
                        sp.dma_start(stk[s][HD * n:HD * n + HD, :, :].bitcast(F32),
                                     part[64 * e:64 * e + 64, :].bitcast(F32)).then_inc(stack_ready[s], 16)

            def max_row(b, t):
                sp.wait_ge(mneg_ready, b * QUADS + t + 1)
                sp.dma_start(qstk[t % SLOTS][MROW:MROW + 1, :, :].bitcast(F32),
                             mneg[t % 2][:].bitcast(F32)).then_inc(mrow_ready, 16)

            with sp.Fori(0, B) as b:
                sp.wait_ge(y_ready, b * NT)
                sp.sem_inc(sp_alone, 1)
                sp.dma_start(x_sb[:], x_v[b]).then_inc(x_loaded, 16)
                stack(b, 0)
                stack(b, 1)
                max_row(b, 0)
                for t in range(QUADS):
                    if t + 2 < QUADS:
                        stack(b, t + 2)
                    if t + 1 < QUADS:
                        max_row(b, t + 1)
                sp.wait_ge(y_ready, b * NT + NT)
                sp.sem_inc(sp_alone, 1)
                sp.dma_start(out_v[b], y_sb[:]).then_inc(stored, 16)
            sp.wait_ge(stored, 16 * B)

        @block.gpsimd
        def _(g):
            for src, dst in ((bq, bq_sb), (bk, bk_sb)):
                g.dma_start(dst[:], src).then_inc(bias_loaded, 16)
            for src, dst in ((bv, bv_sb), (bo, bo_sb)):
                g.dma_start(dst[:], src.partition_broadcast(P)).then_inc(bias_loaded, 16)
            n = 0

            def step(i):
                nonlocal n
                n += 1
                i.then_inc(const_ready, 1)
                g.wait_ge(const_ready, n)
            step(nc.gpsimd.memset(ident[:], 0.0))
            step(nc.gpsimd.affine_select(out=ident[:], in_=ident[:], compare_op=ALU.not_equal, fill=1.0,
                                         base=0, pattern=[[-1, P]], channel_multiplier=1))
            step(nc.gpsimd.tensor_copy(ident_b[:], ident[:]))
            step(nc.gpsimd.memset(ones[:], 0.0))
            step(nc.gpsimd.affine_select(out=future[:], in_=ones[:], compare_op=ALU.is_ge, fill=NEG,
                                         base=0, pattern=[[-1, P]], channel_multiplier=1))
            step(nc.gpsimd.memset(ones[:], 1.0))
            step(nc.gpsimd.memset(minus_half[:], -0.5))
            step(nc.gpsimd.memset(absum[:], 0.0))
            step(nc.gpsimd.memset(is_odd[:], 0.0))
            for k in range(P // 32):
                step(nc.gpsimd.affine_select(out=is_odd[:], in_=is_odd[:], compare_op=ALU.is_gt, fill=1.0,
                                             base=32 * k + 16, pattern=[[0, 1]], channel_multiplier=-1))
                step(nc.gpsimd.affine_select(out=is_odd[:], in_=is_odd[:], compare_op=ALU.is_gt, fill=0.0,
                                             base=32 * k + 32, pattern=[[0, 1]], channel_multiplier=-1))
            step(nc.gpsimd.tensor_scalar(is_even[:], is_odd[:], -1.0, 1.0, ALU.mult, ALU.add))

            g.wait_ge(bias_loaded, 64)
            g.wait_ge(setup_done, 1)
            for s in range(SLOTS):
                for stk in (qstk, kstk):
                    step(nc.gpsimd.memset(stk[s][64:MROW, :, :].bitcast(F32), 0.0))
                step(nc.gpsimd.memset(kstk[s][MROW:MROW + 1, :, :].bitcast(F32), 1.0))
            step(nc.gpsimd.memset(v_aug[:], 1.0))

            def alone():
                g.sem_inc(pool_alone, 1)

            def rsqrt(b, k, scale):
                g.wait_ge(mv_ready, b * 2 * NT + k * NT + NT)
                alone()
                nc.gpsimd.tensor_scalar(rstd[:, :, 0], mv[:, :, 1], EPS, None, ALU.add).then_inc(rstd_step, 1)
                g.wait_ge(rstd_step, b * 3 + k + 1)
                if scale is None:
                    nc.gpsimd.tensor_tensor(rstd[:, :, 0], rstd[:, :, 0], minus_half[:], ALU.pow).then_inc(rstd_ready, 1)
                else:
                    nc.gpsimd.tensor_tensor(rstd[:, :, 0], rstd[:, :, 0], minus_half[:], ALU.pow).then_inc(rstd_step, 1)
                    g.wait_ge(rstd_step, b * 3 + 3)
                    alone()
                    nc.gpsimd.tensor_scalar(rstd[:, :, 0], rstd[:, :, 0], scale, None, ALU.mult).then_inc(rstd_ready, 1)

            with g.Fori(0, B) as b:
                rsqrt(b, 0, None)
                g.wait_ge(xn_ready, b * 2 * NT + NT)
                for tt in range(NT):
                    nc.gpsimd.tensor_tensor(x_sb[:, tt, :], x_sb[:, tt, :], bo_sb[:], ALU.add).then_inc(xbo_ready, 1)
                for t in range(QUADS):
                    for h in range(QH):
                        for f, (seg, blocks) in enumerate(((0, 1), (1, 1), (3, 2))):
                            g.wait_ge(exp_done, b * FILLS + 3 * (QH * t + h) + f + 1)
                            alone()
                            at = SEG[seg][0]
                            if blocks == 1:
                                v = probs[:, h, at:at + P]
                                nc.gpsimd.affine_select(out=v, in_=v, compare_op=ALU.is_ge, fill=0.0, base=0,
                                                        pattern=[[1, P]], channel_multiplier=-1).then_inc(probs_masked, 1)
                            else:
                                v = probs[:, h, at:at + 2 * P].rearrange("p (a q) -> p a q", a=2)
                                nc.gpsimd.affine_select(out=v, in_=v, compare_op=ALU.is_ge, fill=0.0, base=0,
                                                        pattern=[[0, 2], [1, P]], channel_multiplier=-1).then_inc(probs_masked, 1)
                    if t % 2:
                        blk = t // 2
                        g.wait_ge(den_step, b * BLOCKS + blk + 1)
                        nc.gpsimd.tensor_tensor(aT[:, blk, :], num[:], rden[:], ALU.mult).then_inc(aT_ready, 1)
                rsqrt(b, 1, X2_SCALE)

        @block.scalar
        def _(a):
            act = nc.scalar
            a.wait_ge(const_ready, 8)
            for n, (raw, t) in enumerate(((wg_raw, tg), (wu_raw, tu))):
                a.wait_ge(ffnw_loaded[n], 16)
                act.activation(t[:], raw[:], ACT.Abs, accum_out=absum[:, n:n + 1]).then_inc(abs_done, 1)
            a.wait_ge(ffnw_loaded[2], 32)
            act.activation(td[:, 0:NI - 1, :], wd_raw[:, 0:NI - 1, :], ACT.Abs, accum_out=absum[:, 2:3]).then_inc(abs_done, 1)
            act.activation(td[0:IR, NI - 1, :], wd_raw[0:IR, NI - 1, :], ACT.Abs, accum_out=absum[0:IR, 3:4]).then_inc(abs_done, 1)
            a.wait_ge(bias_loaded, 64)
            act.mul(bq_sb[:], bq_sb[:], HD ** -0.5).then_inc(bq_ready, 1)
            a.wait_ge(bq_ready, 1)

            def copy_qk(b, kind, blk):
                n = UNIT[kind, blk]
                a.wait_ge(unit_ready, b * len(UNITS) + n + 1)
                a.wait_ge(split_done, b * 4 * BLOCKS + 4 * blk)
                bank = 2 * (n % 2)
                if kind == "q":
                    act.activation(qf[:], ps[:, bank, :], ACT.Identity, bias=bq_sb[:, blk:blk + 1],
                                   scale=HD ** -0.5).then_inc(qkf_ready, 1)
                else:
                    act.activation(kf[:], ps[:, bank, :], ACT.Identity, bias=bk_sb[:, blk:blk + 1]).then_inc(qkf_ready, 1)

            def copy_max(b, t):
                n = UNIT["m", t]
                a.wait_ge(unit_ready, b * len(UNITS) + n + 1)
                a.wait_ge(mrow_ready, b * 16 * QUADS + 16 * max(t - 1, 0))
                act.activation(mneg[t % 2][:], ps[0:QH, 2 * (n % 2), :], ACT.Copy, scale=-1.0).then_inc(mneg_ready, 1)

            def exps(b, t, h, f):
                n = 3 * (QH * t + h) + f
                a.wait_ge(scores_ready, b * FILLS + n + 1)
                if h == 0 and f == 0:
                    a.wait_ge(pv_done, b * QUADS + t)
                lo, hi = ((0, 512), (0, 384), (128, 512))[f]
                at = SEG[(0, 1, 3)[f]][0]
                act.activation(probs[:, h, at:at + hi - lo], ps[:, 4 + n % 2, lo:hi], ACT.Exp).then_inc(exp_done, 1)

            with a.Fori(0, B) as b:
                for c in (0, 1):
                    a.wait_ge(xT_ps, b * 2 * NC + c + 1)
                    act.activation(xT[:, c, :], ps[:, c, :], ACT.Copy).then_inc(xT_act, 1)
                copy_qk(b, "q", 0)
                copy_qk(b, "k", 0)
                copy_max(b, 0)
                for t in range(QUADS):
                    if t % 2 == 0 and t // 2 + 1 < BLOCKS:
                        copy_qk(b, "q", t // 2 + 1)
                        copy_qk(b, "k", t // 2 + 1)
                    for h in range(QH):
                        for f in range(3):
                            exps(b, t, h, f)
                    if t + 1 < QUADS:
                        copy_max(b, t + 1)
                    if t % 2:
                        blk = t // 2
                        a.wait_ge(pv_done, b * QUADS + t + 1)
                        a.wait_ge(norm_dve, b * 2 * BLOCKS + 2 * blk)
                        act.activation(even_num[:], ps[:, 6, :], ACT.Copy, scale=is_even[:]).then_inc(even_parts, 1)
                        act.activation(even_den[:], ps[:, 6, :], ACT.Copy, scale=is_odd[:]).then_inc(even_parts, 1)
                for c in range(NC):
                    a.wait_ge(xT_ps, b * 2 * NC + NC + c + 1)
                    act.activation(x2h[:, c, :], ps[:, 4 + c, :], ACT.Copy).then_inc(x2h_ready, 1)
                for ch in range(NI):
                    m = P if ch < NI - 1 else IR
                    a.wait_ge(gu_ps, b * NI + ch + 1)
                    if ch >= 2:
                        a.wait_ge(inter_ready, b * NI + ch - 1)
                    act.activation(gate_s[ch % 2][0:m, :], ps[0:m, 2 * (ch % 2), :], ACT.Copy,
                                   scale=INTER_SCALE).then_inc(gate_ready, 1)
                    a.wait_ge(inter_ready, b * NI + ch + 1)
                    act.activation(ih[0:m, ch, :], inter[ch % 2][0:m, :], ACT.Copy).then_inc(ih_ready, 1)

        @block.vector
        def _(v):
            dve = nc.vector
            v.wait_ge(sums_ready, 1)
            counts = (D * I, D * I, D * I)
            st = [0]

            def step(i):
                st[0] += 1
                i.then_inc(tern, 1)
                v.wait_ge(tern, st[0])
            step(dve.tensor_copy(wscale[:, 0:2], ps[:, 0, 0:2]))
            step(dve.tensor_copy(wscale[:, 2:3], ps[:, 0, 2:3]))
            step(dve.tensor_tensor(wscale[:, 2:3], ps[:, 0, 3:4], wscale[:, 2:3], ALU.add))
            step(dve.tensor_scalar(wscale[:], wscale[:], 1.0 / counts[0], None, ALU.mult))
            step(dve.tensor_scalar(wthr[:], wscale[:], EPS, 0.5, ALU.add, ALU.mult))
            step(dve.tensor_scalar(wnthr[:], wthr[:], -1.0, None, ALU.mult))
            step(dve.tensor_tensor(fscale[:, 0:1], wscale[:, 0:1], wscale[:, 1:2], ALU.mult))
            step(dve.scalar_tensor_tensor(out=fscale[:, 1:2], in0=fscale[:, 0:1], scalar=OUT_SCALE,
                                          in1=wscale[:, 2:3], op0=ALU.mult, op1=ALU.mult))
            for n, (raw, t, rows, cols) in enumerate(((wg_raw, tg, P, NC), (wu_raw, tu, P, NC), (wd_raw, td, P, NI - 1), (wd_raw, td, IR, NI))):
                r, k = (slice(0, rows), slice(0, cols)) if n < 3 else (slice(0, rows), slice(NI - 1, NI))
                w = min(n, 2)
                step(dve.tensor_scalar(t[r, k, :], raw[r, k, :], wnthr[r, w:w + 1], None, ALU.is_lt))
                i = dve.scalar_tensor_tensor(out=t[r, k, :], in0=raw[r, k, :], scalar=wthr[r, w:w + 1], in1=t[r, k, :],
                                             op0=ALU.is_gt, op1=ALU.subtract)
                if n < 3:
                    step(i)
                else:
                    i.then_inc(setup_done, 1)
            v.wait_ge(setup_done, 1)
            v.wait_ge(bias_loaded, 64)
            v.wait_ge(const_ready, CONSTS)

            def norm(b, k, dst):
                for tt in range(NT):
                    if k == 1:
                        v.wait_ge(x1_ready, b * NT + tt + 1)
                    dve.bn_stats(stats[:, tt, :], x_sb[:, tt, :]).then_inc(split_step, 1)
                for tt in range(NT):
                    v.wait_ge(split_step, b * SS + k * NT + tt + 1)
                    v.sem_inc(dve_alone, 1)
                    dve.bn_aggr(mv[:, tt, :], stats[:, tt, :]).then_inc(mv_ready, 1)
                v.wait_ge(rstd_ready, 2 * b + k + 1)
                for tt in range(NT):
                    dve.tensor_scalar(dst[:, tt, :], x_sb[:, tt, :], mv[:, tt, 0:1], rstd[:, tt, :],
                                      ALU.subtract, ALU.mult).then_inc(xn_ready, 1)

            SS = 2 * NT

            def split(b, blk):
                for j, (full, hi, lo) in enumerate(((qf, qh, ql), (kf, kh, kl))):
                    v.wait_ge(qkf_ready, b * 2 * BLOCKS + 2 * blk + j + 1)
                    if blk:
                        for s in range(SLOTS):
                            last = max(t for t in range(2 * blk) if t % SLOTS == s) if s < 2 * blk else None
                            if last is not None:
                                v.wait_ge(stack_ready[s], b * 128 * USES[s] + 128 * (last // SLOTS + 1))
                    dve.tensor_copy(hi[:], full[:]).then_inc(split_done, 1)
                    v.wait_ge(split_done, b * 4 * BLOCKS + 4 * blk + 2 * j + 1)
                    dve.tensor_tensor(lo[:], full[:], hi[:].bitcast(F32), ALU.subtract).then_inc(split_done, 1)

            USES = [len(range(s, QUADS, SLOTS)) for s in range(SLOTS)]

            def free(n):
                return unit_free[n % 2]

            def maxima(b, t, p):
                for u in range(3):
                    n = UNIT["max", t, p, u]
                    v.wait_ge(unit_ready, b * len(UNITS) + n + 1)
                    if p == 0 and u == 0 and t >= 2:
                        v.wait_ge(unit_ready, b * len(UNITS) + UNIT["m", t - 2] + 1)
                    bank = 2 * (n % 2)
                    rows = ((3, 0, 512),), ((2, 0, 384),), ((1, 0, 256), (0, 256, 384))
                    for i, lo, hi in rows[u]:
                        r = dve.reduce_max(mx[t % 2][:, i, 2 * p:2 * p + 2], ps[:, bank:bank + 2, lo:hi], AX.X)
                        r.then_inc(max_ready, 1)

            with v.Fori(0, B) as b:
                v.wait_ge(x_loaded, 16 * b + 16)
                norm(b, 0, xn)
                for c in (2, 3):
                    v.wait_ge(xT_ps, b * 2 * NC + c + 1)
                    dve.tensor_copy(xT[:, c, :], ps[:, c, :]).then_inc(xT_dve, 1)
                for tt in range(NT):
                    v.wait_ge(v_ps, b * NT + tt + 1)
                    for e in range(2):
                        dve.tensor_tensor(v_aug[:, tt, :, 48 * e:48 * e + HD],
                                          ps[:, 4 + tt, :].rearrange("p (j e r) -> p j e r", e=2, r=HD)[:, :, e, :],
                                          bv_sb[:].rearrange("p (j e r) -> p j e r", e=2, r=HD)[:, :, e, :],
                                          ALU.add).then_inc(v_ready, 1)
                split(b, 0)
                maxima(b, 0, 0)
                maxima(b, 0, 1)
                for t in range(QUADS):
                    if t % 2 == 0 and t // 2 + 1 < BLOCKS:
                        split(b, t // 2 + 1)
                    if t + 1 < QUADS:
                        maxima(b, t + 1, 0)
                        maxima(b, t + 1, 1)
                    if t % 2:
                        blk = t // 2
                        v.wait_ge(even_parts, b * 2 * BLOCKS + 2 * blk + 2)
                        if blk:
                            v.wait_ge(aT_ready, b * BLOCKS + blk)
                        dve.scalar_tensor_tensor(out=den_far[:], in0=ps[:, 7, :], scalar=is_even[:], in1=even_den[:],
                                                 op0=ALU.mult, op1=ALU.add).then_inc(norm_dve, 1)
                        dve.scalar_tensor_tensor(out=num[:], in0=ps[:, 7, :], scalar=is_odd[:], in1=even_num[:],
                                                 op0=ALU.mult, op1=ALU.add).then_inc(norm_dve, 1)
                        v.wait_ge(norm_dve, b * 2 * BLOCKS + 2 * blk + 2)
                        v.sem_inc(dve_alone, 1)
                        dve.stream_shuffle(den[:], den_far[:], [(i + HD) % 32 for i in range(32)]).then_inc(den_moved, 1)
                        v.wait_ge(den_moved, b * BLOCKS + blk + 1)
                        dve.reciprocal(rden[:], den[:]).then_inc(den_step, 1)
                for tt in range(NT):
                    v.wait_ge(wo_ps, b * NT + tt + 1)
                    v.wait_ge(xbo_ready, b * NT + tt + 1)
                    dve.tensor_tensor(x_sb[:, tt, :], ps[:, tt, :], x_sb[:, tt, :], ALU.add).then_inc(x1_ready, 1)
                norm(b, 1, xn2)
                for c in range(NC):
                    v.wait_ge(x2h_ready, b * NC + c + 1)
                    dve.tensor_tensor(x2l[:, c, :], ps[:, 4 + c, :], x2h[:, c, :], ALU.subtract).then_inc(x2l_ready, 1)
                for ch in range(NI):
                    m = P if ch < NI - 1 else IR
                    v.wait_ge(gate_ready, b * NI + ch + 1)
                    if ch >= 2:
                        v.wait_ge(ih_ready, b * NI + ch - 1)
                    dve.tensor_tensor(inter[ch % 2][0:m, :], ps[0:m, 2 * (ch % 2) + 1, :], gate_s[ch % 2][0:m, :],
                                      ALU.mult).then_inc(inter_ready, 1)
                    v.wait_ge(ih_ready, b * NI + ch + 1)
                    dve.tensor_tensor(il[0:m, ch, :], inter[ch % 2][0:m, :], ih[0:m, ch, :], ALU.subtract).then_inc(il_ready, 1)
                v.wait_ge(stored, 16 * b)
                for tt in range(NT):
                    v.wait_ge(down_ps, b * NT + tt + 1)
                    dve.scalar_tensor_tensor(out=y_sb[:, tt, :], in0=ps[:, 4 + tt, :], scalar=fscale[:, 1:2],
                                             in1=x_sb[:, tt, :], op0=ALU.mult, op1=ALU.add).then_inc(y_ready, 1)

        @block.tensor
        def _(pe):
            mm = nc.tensor.matmul
            pe.wait_ge(abs_done, 4)
            pe.wait_ge(const_ready, 8)
            mm(ps[:, 0, 0:4], ones[:], absum[:], start=True, stop=True).then_inc(sums_ready, 1)
            pe.wait_ge(wqkv_loaded, 48)
            pe.wait_ge(wo_loaded, 16)
            pe.wait_ge(setup_done, 1)

            def unit(b, u):
                n = UNIT[u]
                if n >= 2:
                    pe.wait_ge(*unit_used(b, n - 2))
                return 2 * (n % 2)

            reads = {}
            counts = {"qk": 0, "m": 0, "max": 0}
            for n, u in enumerate(UNITS):
                if u[0] in "qk":
                    counts["qk"] += 1
                    reads[n] = (qkf_ready, 2 * BLOCKS, counts["qk"])
                elif u[0] == "m":
                    counts["m"] += 1
                    reads[n] = (mneg_ready, QUADS, counts["m"])
                else:
                    counts["max"] += 2 if u[3] == 2 else 1
                    reads[n] = (max_ready, 8 * QUADS, counts["max"])

            def unit_used(b, n):
                s, per_batch, count = reads[n]
                return s, b * per_batch + count

            def project(b, kind, blk):
                bank = unit(b, (kind, blk))
                w = wq_sb if kind == "q" else wk_sb
                for c in range(NC):
                    i = mm(ps[:, bank, :], w[:, c, P * blk:P * blk + P], xT[:, c, :], start=(c == 0), stop=(c == NC - 1))
                i.then_inc(unit_ready, 1)

            def max_unit(b, t, p, u):
                bank = unit(b, ("max", t, p, u))
                s = t % SLOTS
                if p == 0 and u == 0:
                    pe.wait_ge(stack_ready[s], b * 128 * len(range(s, QUADS, SLOTS)) + 128 * (t // SLOTS + 1))
                for hh in range(2):
                    h = 2 * p + hh
                    for qb, at, n in (((3, 0, 512),), ((2, 0, 384),), ((1, 0, 256), (0, 256, 256)))[u]:
                        mm(ps[:, bank + hh, at:at + n], qstk[s][0:MROW, h, P * qb:P * qb + P], kstk[s][0:MROW, h, 0:n],
                           start=True, stop=False)
                        i = mm(ps[:, bank + hh, at + P * qb:at + P * qb + P], ident_b[:], future[:], start=False, stop=True)
                i.then_inc(unit_ready, 1)

            def m_unit(b, t):
                bank = unit(b, ("m", t))
                pe.wait_ge(max_ready, b * 8 * QUADS + 8 * (t + 1))
                for qb in range(NT):
                    i = nc.tensor.transpose(ps[0:QH, bank, P * qb:P * qb + P], mx[t % 2][:, qb, :], ident[:])
                i.then_inc(unit_ready, 1)

            def fill(b, t, h, f):
                n = 3 * (QH * t + h) + f
                if n >= 2:
                    pe.wait_ge(exp_done, b * FILLS + n - 1)
                s = t % SLOTS
                if h == 0 and f == 0:
                    pe.wait_ge(mrow_ready, b * 16 * QUADS + 16 * (t + 1))
                q, k = qstk[s][0:MROW + 1, h, :], kstk[s][0:MROW + 1, h, :]
                bank = 4 + n % 2
                for kb, q0, at in (((0, 0, 0),), ((1, 128, 0),), ((3, 256, 0), (2, 256, 256)))[f]:
                    i = mm(ps[:, bank, at:at + L - q0], k[:, P * kb:P * kb + P], q[:, q0:L], start=True, stop=True)
                i.then_inc(scores_ready, 1)

            def values(b, t):
                blk, e = t // 2, t % 2
                pe.wait_ge(probs_masked, b * FILLS + 3 * QH * (t + 1))
                if e == 0 and blk:
                    pe.wait_ge(norm_dve, b * 2 * BLOCKS + 2 * blk)
                for n, kb in enumerate((0, 1, 3, 2)):
                    at, q0 = SEG[kb]
                    for h in range(QH):
                        i = mm(ps[32 * h:32 * h + 32, 6 + e, q0:L], v_aug[:, kb, QH * blk + h, 32 * e:32 * e + 32],
                               probs[:, h, at:at + L - q0], start=(n == 0), stop=(n == NT - 1))
                i.then_inc(pv_done, 1)

            with pe.Fori(0, B) as b:
                for c in range(NC):
                    if c == 0:
                        pe.wait_ge(xn_ready, b * 2 * NT + NT)
                        pe.wait_ge(y_ready, b * NT)
                    for tt in range(NT):
                        i = nc.tensor.transpose(ps[:, c, P * tt:P * tt + P], xn[:, tt, P * c:P * c + P], ident[:])
                    i.then_inc(xT_ps, 1)
                pe.wait_ge(xT_act, b * 2 + 2)
                pe.wait_ge(xT_dve, b * 2 + 2)
                for tt in range(NT):
                    for c in range(NC):
                        i = mm(ps[:, 4 + tt, :], xT[:, c, P * tt:P * tt + P], wv_sb[:, c, :], start=(c == 0), stop=(c == NC - 1))
                    i.then_inc(v_ps, 1)
                project(b, "q", 0)
                project(b, "k", 0)
                pe.wait_ge(v_ready, b * 2 * NT + 2 * NT)
                pe.wait_ge(const_ready, CONSTS)
                for p in range(2):
                    for u in range(3):
                        max_unit(b, 0, p, u)
                m_unit(b, 0)
                for t in range(QUADS):
                    nxt = [(p, u) for p in range(2) for u in range(3)] if t + 1 < QUADS else []
                    if t % 2 == 0 and t // 2 + 1 < BLOCKS:
                        project(b, "q", t // 2 + 1)
                        project(b, "k", t // 2 + 1)
                    for h in range(QH):
                        for f in range(3):
                            fill(b, t, h, f)
                            if nxt and (3 * h + f) % 2:
                                max_unit(b, t + 1, *nxt.pop(0))
                    if t + 1 < QUADS:
                        m_unit(b, t + 1)
                    values(b, t)
                pe.wait_ge(aT_ready, b * BLOCKS + BLOCKS)
                for tt in range(NT):
                    for c in range(NC):
                        i = mm(ps[:, tt, :], aT[:, c, P * tt:P * tt + P], wo_sb[:, c, :], start=(c == 0), stop=(c == NC - 1))
                    i.then_inc(wo_ps, 1)
                pe.wait_ge(xn_ready, b * 2 * NT + 2 * NT)
                for c in range(NC):
                    for tt in range(NT):
                        i = nc.tensor.transpose(ps[:, 4 + c, P * tt:P * tt + P], xn2[:, tt, P * c:P * c + P], ident[:])
                    i.then_inc(xT_ps, 1)
                pe.wait_ge(x2l_ready, b * NC + NC)

                def down(ch):
                    m = P if ch < NI - 1 else IR
                    pe.wait_ge(il_ready, b * NI + ch + 1)
                    for tt in range(NT):
                        for part in (ih, il):
                            i = mm(ps[:, 4 + tt, :], part[0:m, ch, P * tt:P * tt + P], td[0:m, ch, :],
                                   start=(ch == 0 and part is ih), stop=(ch == NI - 1 and part is il))
                        if ch == NI - 1:
                            i.then_inc(down_ps, 1)
                for ch in range(NI):
                    m = P if ch < NI - 1 else IR
                    if ch >= 2:
                        pe.wait_ge(inter_ready, b * NI + ch - 1)
                    for k, w in enumerate((tg, tu)):
                        for c in range(NC):
                            for part in (x2h, x2l):
                                i = mm(ps[0:m, 2 * (ch % 2) + k, :], w[:, c, P * ch:P * ch + m], part[:, c, :],
                                       start=(c == 0 and part is x2h), stop=(c == NC - 1 and part is x2l))
                    i.then_inc(gu_ps, 1)
                    if ch >= 2:
                        down(ch - 2)
                down(NI - 2)
                down(NI - 1)


CONSTS = 9 + 2 * (P // 32) + 1 + 3 * SLOTS + 1
_INS = ["x", "wq", "bq", "wk", "bk", "wv", "bv", "wo", "bo", "wg", "wu", "wd"]


def kernel(L0_attn_x, L0_attn_Wq, L0_attn_bq, L0_attn_Wk, L0_attn_bk, L0_attn_Wv, L0_attn_bv, L0_attn_Wo, L0_attn_bo,
           L0_ffn_w_gate, L0_ffn_w_up, L0_ffn_w_down):
    import numpy as np
    import concourse.bacc as bacc
    from concourse.bass_utils import run_bass_kernel_spmd

    def rows(w):
        w = np.asarray(w)
        r = w.reshape((BLOCKS, QH, 2, HD) + w.shape[1:])
        return np.ascontiguousarray(np.moveaxis(r, (2, 3, 1), (1, 2, 3)).reshape(w.shape))

    t = lambda w: np.ascontiguousarray(np.asarray(w).T)
    arrays = {
        "x": np.asarray(L0_attn_x), "wq": t(rows(L0_attn_Wq)), "bq": t(rows(L0_attn_bq).reshape(BLOCKS, P)), "wk": t(rows(L0_attn_Wk)),
        "bk": t(rows(L0_attn_bk).reshape(BLOCKS, P)), "wv": t(L0_attn_Wv), "bv": np.asarray(L0_attn_bv), "wo": t(L0_attn_Wo),
        "bo": np.asarray(L0_attn_bo), "wg": t(L0_ffn_w_gate), "wu": t(L0_ffn_w_up), "wd": t(L0_ffn_w_down),
    }
    nc = bacc.Bacc("TRN2", target_bir_lowering=False, num_devices=1)
    aps = [nc.dram_tensor(f"in_{n}", arrays[n].shape, mybir.dt.from_np(arrays[n].dtype), kind="ExternalInput").ap() for n in _INS]
    out = nc.dram_tensor("out", (B, L, D), F32, kind="ExternalOutput").ap()
    preln_block(nc, *aps, out)
    r = run_bass_kernel_spmd(nc, [{f"in_{n}": arrays[n] for n in _INS}], core_ids=[0])
    return r.results[0]["out"]
```

```python
import concourse.bass as bass
from concourse import mybir
from contextlib import ExitStack

F32 = mybir.dt.float32
F32R = mybir.dt.float32r
F16 = mybir.dt.float16
BF16 = mybir.dt.bfloat16
ALU = mybir.AluOpType
ACT = mybir.ActivationFunctionType
AX = mybir.AxisListType

P = 128
B, L, D = 4, 512, 512
H = 32
HD = D // H
I = 1376
NT = L // P
NC = D // P
NI = -(-I // P)
IR = I - (NI - 1) * P
HALF = L // 2
BLOCKS = D // P
QH = 4
QUADS = H // QH
SLOTS = 2
EPS = 1e-5
X2_SCALE = 64.0
INTER_SCALE = 2.0 ** -15
OUT_SCALE = 1.0 / (X2_SCALE * X2_SCALE * INTER_SCALE)
NEG = -1e30
MROW = 96

SEG = {0: (0, 0), 1: (512, 128), 3: (896, 384), 2: (1024, 256)}
PW = 1280
FILLS = 3 * QH
MAXES = 4 * QH

MAX_BANK, DENSE_BANK, SCORE_BANK, SUM_BANK = 0, 2, 4, 6

POS = 20
FILL_AT = {n: n for n in range(FILLS)}
MAX_AT = {n + 3: n for n in range(FILLS)}
M_AT, SUM_AT = 16, 17
STEPS = [
    [("qk", 2), ("qk", 3), ("x2", 0), ("x2", 1), ("gu", 0), ("gu", 1)],
    [("gu", n) for n in range(2, 7)],
    [("qk", 4), ("qk", 5)] + [("gu", n) for n in range(7, 10)],
    [("gu", 10), ("x2", 2), ("x2", 3), ("dn", 0), ("dn", 1)],
    [("qk", 6), ("qk", 7)] + [("gu", n) for n in range(11, 14)],
    [("gu", n) for n in range(14, 19)],
    [("gu", n) for n in range(19, 22)],
    [("dn", 2), ("dn", 3)],
]
PIECES = {"qk": NC, "x2": 1, "gu": NC, "dn": NI}
FFN_KINDS = ("wo", "x2", "gu", "dn")
BEFORE = [("xT", n) for n in range(NC)] + [("qk", 0), ("qk", 1)] + [("v", n) for n in range(NT)]


def has(kind, attn, ffn):
    return ffn if kind in FFN_KINDS else attn


def dense_order(attn, ffn):
    order = BEFORE + [("wo", n) for n in range(NT)] + sum(STEPS, [])
    return [u for u in order if has(u[0], attn, ffn)]


def placed(t, attn, ffn):
    pieces = [(u, c) for u in STEPS[t] if has(u[0], attn, ffn) for c in range(PIECES[u[0]])]
    at = [[] for _ in range(POS)]
    for n, piece in enumerate(pieces):
        at[n * POS // len(pieces)].append(piece)
    return at


def finished(t, attn, ffn):
    return [[u for u, c in pieces if c == PIECES[u[0]] - 1] for pieces in placed(t, attn, ffn)]


RAW = ([(0, c, 1, P, I) for c in range(NC)] + [(1, c, 1, P, I) for c in range(NC)]
       + [(2, c, 2, P, D) for c in range(0, NI - 1, 2)] + [(2, NI - 1, 1, IR, D)])
RAW_RING = 3
SUM_STEPS = {2: (0, 4), 3: (4, 9), 4: (9, 14)}
TERN_STEPS = {5: (0, 5), 6: (5, 10), 7: (10, 14)}


def preln_block(nc, x, wq, bq, wk, bk, wv, bv, wo, bo, wg, wu, wd, out):
    ctx = ExitStack()
    with ctx:
        def sb(name, shape, dt, where=ctx):
            return where.enter_context(nc.sbuf_tensor(name, shape, dt))

        def sem(name):
            return ctx.enter_context(nc.semaphore(name))

        wq_sb = sb("wq_sb", [P, NC, D], F32)
        wk_sb = sb("wk_sb", [P, NC, D], F32)
        wv_sb = sb("wv_sb", [P, NC, D], F32)
        wo_sb = sb("wo_sb", [P, NC, D], F32)
        tg = sb("tg", [P, NC, I], F16)
        tu = sb("tu", [P, NC, I], F16)
        td = sb("td", [P, NI, D], F16)
        bq_sb = sb("bq_sb", [P, BLOCKS], F32)
        bk_sb = sb("bk_sb", [P, BLOCKS], F32)
        bv_sb = sb("bv_sb", [P, D], F32)
        bo_sb = sb("bo_sb", [P, D], F32)
        ident = sb("ident", [P, P], F32)
        ident_b = sb("ident_b", [P, P], BF16)
        future = sb("future", [P, P], BF16)
        ones = sb("ones", [P, P], F32)
        is_even = sb("is_even", [P, 1], F32)
        is_odd = sb("is_odd", [P, 1], F32)
        minus_half = sb("minus_half", [P, NT], F32)
        absum = sb("absum", [P, len(RAW)], F32)
        wscale = sb("wscale", [P, 3], F32)
        wthr = sb("wthr", [P, 3], F32)
        wnthr = sb("wnthr", [P, 3], F32)
        fscale = sb("fscale", [P, 2], F32)
        xa = sb("xa", [P, NT, D], F32)
        xr = sb("xr", [P, NT, D], F32)
        stats = sb("stats", [P, NT, 6], F32)
        mv = sb("mv", [P, NT, 2], F32)
        rstd = sb("rstd", [P, NT, 1], F32)
        xT = sb("xT", [P, NC, L], F32)
        v_aug = sb("v_aug", [P, NT, H // 2, 64], F32)
        qstk = [sb(f"qstk{s}", [P, QH, L], F32R) for s in range(SLOTS)]
        kstk = [sb(f"kstk{s}", [P, QH, L], F32R) for s in range(SLOTS)]
        qk_hi = [sb(f"{n}_hi", [P, L], F32R) for n in "qk"]
        qk_lo = [sb(f"{n}_lo", [P, L], F32R) for n in "qk"]
        mx = [sb(f"mx{s}", [P, NT, QH], F32) for s in range(2)]
        mneg = sb("mneg", [QH, L], F32R)
        probs = sb("probs", [P, QH, PW], F32)
        num = sb("num", [P, L], F32)
        den = sb("den", [P, L], F32)
        aT = sb("aT", [P, BLOCKS, L], F32)
        early = ExitStack()
        raw = [sb(f"raw{s}", [P, I], F32, early) for s in range(RAW_RING)]
        early.close()
        x2h = sb("x2h", [P, NC, HALF], F16)
        x2l = sb("x2l", [P, NC, HALF], F16)
        gate_s = [sb(f"gate_s{s}", [P, HALF], F32) for s in range(2)]
        inter = [sb(f"inter{s}", [P, HALF], F32) for s in range(2)]
        ih = sb("ih", [P, NI, HALF], F16)
        il = sb("il", [P, NI, HALF], F16)

        ps = ctx.enter_context(nc.psum_tensor("ps", [P, 8, 512], F32))

        xa_loaded = sem("xa_loaded")
        xr_loaded = sem("xr_loaded")
        wqk_loaded = sem("wqk_loaded")
        wv_loaded = sem("wv_loaded")
        wo_loaded = sem("wo_loaded")
        bias_loaded = sem("bias_loaded")
        raw_loaded = [sem(f"raw_loaded{s}") for s in range(RAW_RING)]
        const_ready = sem("const_ready")
        raw_summed = sem("raw_summed")
        sums_ready = sem("sums_ready")
        thr_step = sem("thr_step")
        negatives = sem("negatives")
        ternary = sem("ternary")
        stats_ready = sem("stats_ready")
        mv_ready = sem("mv_ready")
        rstd_step = sem("rstd_step")
        rstd_ready = sem("rstd_ready")
        xn_ready = sem("xn_ready")
        xn2_ready = sem("xn2_ready")
        xT_ps = sem("xT_ps")
        xT_act = sem("xT_act")
        xT_dve = sem("xT_dve")
        qk_ps = sem("qk_ps")
        hi_ready = sem("hi_ready")
        lo_ready = sem("lo_ready")
        stack_ready = [sem(f"stack_ready{s}") for s in range(SLOTS)]
        v_ps = sem("v_ps")
        v_ready = sem("v_ready")
        max_ps = sem("max_ps")
        max_ready = sem("max_ready")
        m_ps = sem("m_ps")
        mneg_ready = sem("mneg_ready")
        mrow_ready = sem("mrow_ready")
        scores_ready = sem("scores_ready")
        exp_done = sem("exp_done")
        probs_masked = sem("probs_masked")
        sums_done = sem("sums_done")
        even_parts = sem("even_parts")
        parts_joined = sem("parts_joined")
        den_moved = sem("den_moved")
        rden_ready = sem("rden_ready")
        aT_ready = sem("aT_ready")
        xbo_ready = sem("xbo_ready")
        wo_ps = sem("wo_ps")
        x1_ready = sem("x1_ready")
        x2_ps = sem("x2_ps")
        x2h_ready = sem("x2h_ready")
        x2l_ready = sem("x2l_ready")
        gu_ps = sem("gu_ps")
        gate_ready = sem("gate_ready")
        inter_ready = sem("inter_ready")
        ih_ready = sem("ih_ready")
        il_ready = sem("il_ready")
        dn_ps = sem("dn_ps")
        y_ready = sem("y_ready")
        stored = sem("stored")
        pool_alone = sem("pool_alone")
        dve_alone = sem("dve_alone")
        sp_alone = sem("sp_alone")

        x_v = x.rearrange("b (t p) d -> b p t d", p=P)
        out_v = out.rearrange("b (t p) d -> b p t d", p=P)

        def wait(eng, s, value, carrier=None):
            if isinstance(value, int) and value <= 0:
                return
            eng.wait_ge(s, value)
            if carrier is not None:
                eng.sem_inc(carrier, 1)

        block = ctx.enter_context(nc.Block())

        @block.sync
        def _(sp):
            sp.dma_start(xa[:], x_v[0]).then_inc(xa_loaded, 16)
            for dst, src in ((wq_sb, wq), (wk_sb, wk)):
                sp.dma_start(dst[:], src.rearrange("(c p) n -> p c n", p=P)).then_inc(wqk_loaded, 16)
            sp.dma_start(wv_sb[:], wv.rearrange("(c p) n -> p c n", p=P)).then_inc(wv_loaded, 16)

            def load_raw(n):
                m, c, k, rows, cols = RAW[n % len(RAW)]
                if n >= RAW_RING:
                    wait(sp, raw_summed, min(n - RAW_RING + 1, len(RAW)))
                    wait(sp, ternary, n - RAW_RING + 1 - len(RAW))
                src = (wg, wu, wd)[m]
                src = src[P * c:P * (c + k - 1) + rows, :].rearrange("(k p) n -> p k n", p=rows)
                sp.dma_start(raw[n % RAW_RING][0:rows, 0:k * cols].rearrange("p (k n) -> p k n", k=k), src)\
                  .then_inc(raw_loaded[n % RAW_RING], 16)

            def stack(j, t):
                s, blk, e = t % SLOTS, t // 2, t % 2
                wait(sp, lo_ready, j * 2 * BLOCKS + 2 * blk + 2, sp_alone)
                wait(sp, scores_ready, (j * QUADS + t - SLOTS + 1) * FILLS)
                for n, (qs, ks) in enumerate(((qk_hi[0], qk_hi[1]), (qk_lo[0], qk_hi[1]), (qk_hi[0], qk_lo[1]), (qk_lo[0], qk_lo[1]))):
                    for stk, part in ((qstk, qs), (kstk, ks)):
                        sp.dma_start(stk[s][HD * n:HD * n + HD, :, :].bitcast(F32),
                                     part[64 * e:64 * e + 64, :].bitcast(F32)).then_inc(stack_ready[s], 16)

            def iteration(j, attn, ffn):
                first = isinstance(j, int) and attn
                if attn:
                    stack(j, 0)
                    stack(j, 1)
                if first:
                    for n in range(RAW_RING):
                        load_raw(n)
                    sp.dma_start(xr[:], x_v[0]).then_inc(xr_loaded, 16)
                    sp.dma_start(wo_sb[:], wo.rearrange("(c p) n -> p c n", p=P)).then_inc(wo_loaded, 16)
                for t in range(QUADS):
                    if attn and t + 2 < QUADS:
                        stack(j, t + 2)
                    if first:
                        for lo, hi in (SUM_STEPS.get(t, (0, 0)), TERN_STEPS.get(t, (0, 0))):
                            for n in range(lo, hi):
                                n += len(RAW) * (t in TERN_STEPS) + RAW_RING
                                if n < 2 * len(RAW):
                                    load_raw(n)
                    if attn and t == 4:
                        if ffn:
                            wait(sp, x2_ps, (j - 1) * NT + NT, sp_alone)
                            sp.dma_start(xa[:], x_v[(j + 1) % B]).then_inc(xa_loaded, 16)
                        else:
                            wait(sp, xT_ps, NC)
                            sp.dma_start(xa[:], x_v[1]).then_inc(xa_loaded, 16)
                if ffn:
                    wait(sp, y_ready, j * NT, sp_alone)
                    sp.dma_start(out_v[j - 1], xr[:]).then_inc(stored, 16)
                    wait(sp, stored, 16 * j, sp_alone)
                    if attn:
                        sp.dma_start(xr[:], x_v[j]).then_inc(xr_loaded, 16)

            iteration(0, True, False)
            with sp.Fori(1, B) as j:
                iteration(j, True, True)
            iteration(B, False, True)

        @block.gpsimd
        def _(g):
            pool = nc.gpsimd
            for src, dst in ((bq, bq_sb), (bk, bk_sb)):
                g.dma_start(dst[:], src).then_inc(bias_loaded, 16)
            for src, dst in ((bv, bv_sb), (bo, bo_sb)):
                g.dma_start(dst[:], src.partition_broadcast(P)).then_inc(bias_loaded, 16)
            n_const = 0

            def step(i):
                nonlocal n_const
                n_const += 1
                i.then_inc(const_ready, 1)
                g.wait_ge(const_ready, n_const)
            step(pool.memset(minus_half[:], -0.5))

            def rsqrt(count, scale):
                wait(g, mv_ready, count * NT, pool_alone)
                pool.tensor_scalar(rstd[:, :, 0], mv[:, :, 1], EPS, None, ALU.add).then_inc(rstd_step, 1)
                g.wait_ge(rstd_step, 2 * count - 1)
                pool.tensor_tensor(rstd[:, :, 0], rstd[:, :, 0], minus_half[:], ALU.pow).then_inc(rstd_step, 1)
                wait(g, rstd_step, 2 * count, pool_alone)
                pool.tensor_scalar(rstd[:, :, 0], rstd[:, :, 0], scale, None, ALU.mult).then_inc(rstd_ready, 1)

            rsqrt(1, 1.0)
            step(pool.memset(ident[:], 0.0))
            step(pool.affine_select(out=ident[:], in_=ident[:], compare_op=ALU.not_equal, fill=1.0,
                                    base=0, pattern=[[-1, P]], channel_multiplier=1))
            step(pool.tensor_copy(ident_b[:], ident[:]))
            step(pool.memset(ones[:], 0.0))
            step(pool.affine_select(out=future[:], in_=ones[:], compare_op=ALU.is_ge, fill=NEG,
                                    base=0, pattern=[[-1, P]], channel_multiplier=1))
            step(pool.memset(ones[:], 1.0))
            step(pool.memset(absum[:], 0.0))
            step(pool.memset(is_odd[:], 0.0))
            for k in range(P // 32):
                step(pool.affine_select(out=is_odd[:], in_=is_odd[:], compare_op=ALU.is_gt, fill=1.0,
                                        base=32 * k + 16, pattern=[[0, 1]], channel_multiplier=-1))
                step(pool.affine_select(out=is_odd[:], in_=is_odd[:], compare_op=ALU.is_gt, fill=0.0,
                                        base=32 * k + 32, pattern=[[0, 1]], channel_multiplier=-1))
            step(pool.tensor_scalar(is_even[:], is_odd[:], -1.0, 1.0, ALU.mult, ALU.add))
            for s in range(SLOTS):
                for stk in (qstk, kstk):
                    step(pool.memset(stk[s][64:MROW, :, :].bitcast(F32), 0.0))
                step(pool.memset(kstk[s][MROW:MROW + 1, :, :].bitcast(F32), 1.0))
            step(pool.memset(v_aug[:], 1.0))
            assert n_const == CONSTS
            g.wait_ge(bias_loaded, 64)

            def mask(j, t, n):
                h, f = divmod(n, 3)
                wait(g, exp_done, (j * QUADS + t) * FILLS + n + 1, pool_alone)
                at = SEG[(0, 1, 3)[f]][0]
                k = (1, 1, 2)[f]
                v = probs[:, h, at:at + k * P].rearrange("p (a q) -> p a q", a=k)
                pool.affine_select(out=v, in_=v, compare_op=ALU.is_ge, fill=0.0, base=0,
                                   pattern=[[0, k], [1, P]], channel_multiplier=-1).then_inc(probs_masked, 1)

            def divide(j, blk):
                wait(g, rden_ready, j * BLOCKS + blk + 1)
                if blk == 0:
                    wait(g, wo_ps, j * NT)
                pool.tensor_tensor(aT[:, blk, :], num[:], den[:], ALU.mult).then_inc(aT_ready, 1)

            def parts(i, n):
                half, ch = divmod(n, NI)
                m = P if ch < NI - 1 else IR
                wait(g, inter_ready, i * 2 * NI + n + 1)
                g.sem_inc(pool_alone, 1)
                pool.tensor_copy(ih[0:m, ch, :], inter[n % 2][0:m, :]).then_inc(ih_ready, 1)
                wait(g, ih_ready, i * 2 * NI + n + 1)
                pool.tensor_tensor(il[0:m, ch, :], inter[n % 2][0:m, :], ih[0:m, ch, :], ALU.subtract).then_inc(il_ready, 1)

            def iteration(j, attn, ffn):
                first = isinstance(j, int) and attn
                if ffn:
                    divide(j - 1, BLOCKS - 1)
                    wait(g, xr_loaded, 16 * j)
                    for tt in range(NT):
                        pool.tensor_tensor(xr[:, tt, :], xr[:, tt, :], bo_sb[:], ALU.add).then_inc(xbo_ready, 1)
                    rsqrt(2 * j + 1, X2_SCALE)
                for t in range(QUADS):
                    done = finished(t, attn, ffn)
                    for pos in range(POS):
                        if attn and pos in FILL_AT:
                            mask(j, t, FILL_AT[pos])
                        for kind, n in done[pos]:
                            if kind == "gu":
                                parts(j - 1, n)
                        if attn and pos == 4 and t % 2 == 0 and t:
                            divide(j, t // 2 - 1)
                    if first and t in TERN_STEPS:
                        for n in range(*TERN_STEPS[t]):
                            m, c, k, rows, cols = RAW[n]
                            l = n + len(RAW)
                            wait(g, raw_loaded[l % RAW_RING], 16 * (l // RAW_RING + 1))
                            wait(g, thr_step, THR_STEPS)
                            pool.tensor_scalar((tg, tu, td)[m][0:rows, c:c + k, :],
                                               raw[l % RAW_RING][0:rows, 0:k * cols].rearrange("p (k n) -> p k n", k=k),
                                               wnthr[0:rows, m:m + 1], None, ALU.is_lt).then_inc(negatives, 1)
                    if attn and t == 6:
                        rsqrt(2 * j + 2, 1.0)

            iteration(0, True, False)
            with g.Fori(1, B) as j:
                iteration(j, True, True)
            iteration(B, False, True)

        @block.scalar
        def _(a):
            act = nc.scalar

            def high_part(j, n):
                blk, k = divmod(n, 2)
                wait(a, qk_ps, j * 2 * BLOCKS + n + 1)
                for s in range(SLOTS):
                    wait(a, stack_ready[s], 128 * (j * QUADS // SLOTS + blk))
                act.activation(qk_hi[k][:], ps[:, dense_bank["qk", n], :], ACT.Identity,
                               bias=(bq_sb, bk_sb)[k][:, blk:blk + 1]).then_inc(hi_ready, 1)

            def max_row(j, t):
                wait(a, m_ps, j * QUADS + t + 1)
                wait(a, mrow_ready, 16 * (j * QUADS + t))
                act.activation(mneg[:], ps[0:QH, m_bank(t), :], ACT.Copy, scale=-1.0).then_inc(mneg_ready, 1)
                wait(a, mneg_ready, j * QUADS + t + 1)
                a.dma_start(qstk[t % SLOTS][MROW:MROW + 1, :, :].bitcast(F32), mneg[:].bitcast(F32)).then_inc(mrow_ready, 16)

            def exps(j, t, n):
                h, f = divmod(n, 3)
                wait(a, scores_ready, (j * QUADS + t) * FILLS + n + 1)
                if n == 0:
                    wait(a, sums_done, j * QUADS + t)
                lo, hi = ((0, 512), (0, 384), (128, 512))[f]
                at = SEG[(0, 1, 3)[f]][0]
                act.activation(probs[:, h, at:at + hi - lo], ps[:, SCORE_BANK + n % 2, lo:hi], ACT.Exp,
                               scale=HD ** -0.5).then_inc(exp_done, 1)

            def even_heads(j, blk):
                wait(a, sums_done, j * QUADS + 2 * blk + 2)
                wait(a, aT_ready, j * BLOCKS + blk)
                act.activation(num[:], ps[:, SUM_BANK, :], ACT.Copy, scale=is_even[:]).then_inc(even_parts, 1)
                act.activation(den[:], ps[:, SUM_BANK, :], ACT.Copy, scale=is_odd[:]).then_inc(even_parts, 1)

            def gate(i, n):
                m = P if n % NI < NI - 1 else IR
                wait(a, gu_ps, i * 2 * NI + n + 1)
                if n >= 2:
                    wait(a, inter_ready, i * 2 * NI + n - 1)
                act.activation(gate_s[n % 2][0:m, :], ps[0:m, dense_bank["gu", n], 0:HALF], ACT.Copy,
                               scale=INTER_SCALE).then_inc(gate_ready, 1)

            def x2_high(i, n):
                wait(a, x2_ps, i * NT + n + 1)
                c = 2 * (n % 2)
                act.activation(x2h[:, c:c + 2, :], ps[:, dense_bank["x2", n], :].rearrange("p (c t) -> p c t", c=2),
                               ACT.Copy).then_inc(x2h_ready, 1)

            def iteration(j, attn, ffn):
                first = isinstance(j, int) and attn
                if attn:
                    for c in (0, 1):
                        wait(a, xT_ps, j * NC + c + 1)
                        act.activation(xT[:, c, :], ps[:, dense_bank["xT", c], :], ACT.Copy).then_inc(xT_act, 1)
                    high_part(j, 0)
                    high_part(j, 1)
                if ffn:
                    even_heads(j - 1, BLOCKS - 1)
                if attn:
                    max_row(j, 0)
                for t in range(QUADS):
                    done = finished(t, attn, ffn)
                    for pos in range(POS):
                        if attn and pos in FILL_AT:
                            exps(j, t, FILL_AT[pos])
                        for kind, n in done[pos]:
                            if kind == "qk":
                                high_part(j, n)
                            elif kind == "x2":
                                x2_high(j - 1, n)
                            elif kind == "gu":
                                gate(j - 1, n)
                        if attn and pos == 2 and t % 2 == 0 and t:
                            even_heads(j, t // 2 - 1)
                        if attn and pos == M_AT and t + 1 < QUADS:
                            max_row(j, t + 1)
                    if first and t in SUM_STEPS:
                        for n in range(*SUM_STEPS[t]):
                            m, c, k, rows, cols = RAW[n]
                            a.wait_ge(raw_loaded[n % RAW_RING], 16 * (n // RAW_RING + 1))
                            act.activation((tg, tu, td)[m][0:rows, c:c + k, :],
                                           raw[n % RAW_RING][0:rows, 0:k * cols].rearrange("p (k n) -> p k n", k=k),
                                           ACT.Abs, accum_out=absum[0:rows, n:n + 1]).then_inc(raw_summed, 1)

            a.wait_ge(bias_loaded, 64)
            a.wait_ge(const_ready, CONSTS)
            dense_bank = banks(True, False)
            iteration(0, True, False)
            dense_bank = banks(True, True)
            with a.Fori(1, B) as j:
                iteration(j, True, True)
            dense_bank = banks(False, True)
            iteration(B, False, True)

        @block.vector
        def _(v):
            dve = nc.vector

            def moments(count):
                for tt in range(NT):
                    wait(v, stats_ready, (count - 1) * NT + tt + 1, dve_alone)
                    dve.bn_aggr(mv[:, tt, :], stats[:, tt, :]).then_inc(mv_ready, 1)

            def normalise(count, src, dst, ready):
                wait(v, rstd_ready, count)
                for tt in range(NT):
                    dve.tensor_scalar(dst[:, tt, :], src[:, tt, :], mv[:, tt, 0:1], rstd[:, tt, :],
                                      ALU.subtract, ALU.mult).then_inc(ready, 1)

            def low_part(j, n):
                blk, k = divmod(n, 2)
                wait(v, hi_ready, j * 2 * BLOCKS + n + 1)
                dve.scalar_tensor_tensor(out=qk_lo[k][:], in0=ps[:, dense_bank["qk", n], :],
                                         scalar=(bq_sb, bk_sb)[k][:, blk:blk + 1], in1=qk_hi[k][:].bitcast(F32),
                                         op0=ALU.add, op1=ALU.subtract).then_inc(lo_ready, 1)

            def maxima(j, t, n):
                h, u = divmod(n, 3)
                wait(v, max_ps, (j * QUADS + t) * FILLS + n + 1)
                for i, lo, hi in (((3, 0, 512),), ((2, 0, 384),), ((1, 0, 256), (0, 256, 384)))[u]:
                    dve.reduce_max(mx[t % 2][:, i, h:h + 1], ps[:, max_bank(t, n), lo:hi], AX.X).then_inc(max_ready, 1)

            def join(j, blk):
                wait(v, even_parts, j * 2 * BLOCKS + 2 * blk + 2)
                dve.scalar_tensor_tensor(out=den[:], in0=ps[:, SUM_BANK + 1, :], scalar=is_even[:], in1=den[:],
                                         op0=ALU.mult, op1=ALU.add).then_inc(parts_joined, 1)
                dve.scalar_tensor_tensor(out=num[:], in0=ps[:, SUM_BANK + 1, :], scalar=is_odd[:], in1=num[:],
                                         op0=ALU.mult, op1=ALU.add).then_inc(parts_joined, 1)
                wait(v, parts_joined, j * 2 * BLOCKS + 2 * blk + 2, dve_alone)
                dve.stream_shuffle(den[:], den[:], [(i + HD) % 32 for i in range(32)]).then_inc(den_moved, 1)
                wait(v, den_moved, j * BLOCKS + blk + 1)
                dve.reciprocal(den[:], den[:]).then_inc(rden_ready, 1)

            def values(j, tt):
                wait(v, v_ps, j * NT + tt + 1)
                for e in range(2):
                    dve.tensor_tensor(v_aug[:, tt, :, 48 * e:48 * e + HD],
                                      ps[:, dense_bank["v", tt], :].rearrange("p (j e r) -> p j e r", e=2, r=HD)[:, :, e, :],
                                      bv_sb[:].rearrange("p (j e r) -> p j e r", e=2, r=HD)[:, :, e, :],
                                      ALU.add).then_inc(v_ready, 1)

            def residual(i, tt):
                wait(v, wo_ps, i * NT + tt + 1)
                wait(v, xbo_ready, i * NT + tt + 1)
                dve.tensor_tensor(xr[:, tt, :], ps[:, dense_bank["wo", tt], :], xr[:, tt, :], ALU.add).then_inc(x1_ready, 1)
                wait(v, x1_ready, i * NT + tt + 1)
                dve.bn_stats(stats[:, tt, :], xr[:, tt, :]).then_inc(stats_ready, 1)

            def product(i, n):
                m = P if n % NI < NI - 1 else IR
                wait(v, gate_ready, i * 2 * NI + n + 1)
                if n >= 2:
                    wait(v, il_ready, i * 2 * NI + n - 1)
                dve.tensor_tensor(inter[n % 2][0:m, :], ps[0:m, dense_bank["gu", n], HALF:], gate_s[n % 2][0:m, :],
                                  ALU.mult).then_inc(inter_ready, 1)

            def x2_low(i, n):
                wait(v, x2h_ready, i * NT + n + 1)
                c = 2 * (n % 2)
                dve.tensor_tensor(x2l[:, c:c + 2, :], ps[:, dense_bank["x2", n], :].rearrange("p (c t) -> p c t", c=2),
                                  x2h[:, c:c + 2, :], ALU.subtract).then_inc(x2l_ready, 1)

            def result(i, tt):
                wait(v, dn_ps, i * NT + tt + 1)
                dve.scalar_tensor_tensor(out=xr[:, tt, :], in0=ps[:, dense_bank["dn", tt], :], scalar=fscale[:, 1:2],
                                         in1=xr[:, tt, :], op0=ALU.mult, op1=ALU.add).then_inc(y_ready, 1)

            n_thr = 0

            def thr(i):
                nonlocal n_thr
                n_thr += 1
                i.then_inc(thr_step, 1)
                v.wait_ge(thr_step, n_thr)

            def thresholds():
                v.wait_ge(sums_ready, 1)
                a = 0
                for m in range(3):
                    k = sum(r[0] == m for r in RAW)
                    thr(dve.reduce_sum(wscale[:, m:m + 1], ps[:, MAX_BANK + 1, a:a + k], AX.X))
                    a += k
                thr(dve.tensor_scalar(wscale[:], wscale[:], 1.0 / (D * I), None, ALU.mult))
                thr(dve.tensor_scalar(wthr[:], wscale[:], EPS, 0.5, ALU.add, ALU.mult))
                thr(dve.tensor_scalar(wnthr[:], wthr[:], -1.0, None, ALU.mult))
                thr(dve.tensor_tensor(fscale[:, 0:1], wscale[:, 0:1], wscale[:, 1:2], ALU.mult))
                thr(dve.scalar_tensor_tensor(out=fscale[:, 1:2], in0=fscale[:, 0:1], scalar=OUT_SCALE,
                                             in1=wscale[:, 2:3], op0=ALU.mult, op1=ALU.mult))
                assert n_thr == THR_STEPS

            def make_ternary(n):
                m, c, k, rows, cols = RAW[n]
                l = n + len(RAW)
                t = (tg, tu, td)[m][0:rows, c:c + k, :]
                v.wait_ge(negatives, n + 1)
                dve.scalar_tensor_tensor(out=t, in0=raw[l % RAW_RING][0:rows, 0:k * cols].rearrange("p (k n) -> p k n", k=k),
                                         scalar=wthr[0:rows, m:m + 1], in1=t, op0=ALU.is_gt, op1=ALU.subtract).then_inc(ternary, 1)

            def iteration(j, attn, ffn):
                first = isinstance(j, int) and attn
                if attn:
                    for c in (2, 3):
                        wait(v, xT_ps, j * NC + c + 1)
                        dve.tensor_copy(xT[:, c, :], ps[:, dense_bank["xT", c], :]).then_inc(xT_dve, 1)
                    low_part(j, 0)
                    low_part(j, 1)
                if ffn:
                    join(j - 1, BLOCKS - 1)
                if attn:
                    for tt in range(NT):
                        values(j, tt)
                for tt in range(NT):
                    if ffn:
                        residual(j - 1, tt)
                    if attn:
                        for n in range(3 * tt, 3 * tt + 3):
                            maxima(j, 0, n)
                if ffn:
                    moments(2 * j + 1)
                    normalise(2 * j + 1, xr, xa, xn2_ready)
                for t in range(QUADS):
                    done = finished(t, attn, ffn)
                    if first and t == 5:
                        thresholds()
                    for pos in range(POS):
                        if attn and pos in MAX_AT and t + 1 < QUADS:
                            maxima(j, t + 1, MAX_AT[pos])
                        for kind, n in done[pos]:
                            if kind == "qk":
                                low_part(j, n)
                            elif kind == "x2":
                                x2_low(j - 1, n)
                            elif kind == "gu":
                                product(j - 1, n)
                            elif kind == "dn":
                                result(j - 1, n)
                        if attn and pos == 2 and t % 2 == 0 and t:
                            join(j, t // 2 - 1)
                    if first and t in TERN_STEPS:
                        for n in range(*TERN_STEPS[t]):
                            make_ternary(n)
                    if attn and t == 5:
                        wait(v, xa_loaded, 16 * (j + 2))
                        for tt in range(NT):
                            dve.bn_stats(stats[:, tt, :], xa[:, tt, :]).then_inc(stats_ready, 1)
                        moments(2 * j + 2)
                if attn:
                    normalise(2 * j + 2, xa, xa, xn_ready)

            v.wait_ge(xa_loaded, 16)
            for tt in range(NT):
                dve.bn_stats(stats[:, tt, :], xa[:, tt, :]).then_inc(stats_ready, 1)
            moments(1)
            normalise(1, xa, xa, xn_ready)
            v.wait_ge(bias_loaded, 64)
            v.wait_ge(const_ready, CONSTS)
            dense_bank = banks(True, False)
            iteration(0, True, False)
            dense_bank = banks(True, True)
            with v.Fori(1, B) as j:
                iteration(j, True, True)
            dense_bank = banks(False, True)
            iteration(B, False, True)

        @block.tensor
        def _(pe):
            mm = nc.tensor.matmul

            def read_by(j, u):
                kind, n = u
                i = j - 1
                return {
                    "xT": lambda: (xT_act, j * 2 + n + 1) if n < 2 else (xT_dve, j * 2 + n - 1),
                    "qk": lambda: (lo_ready, j * 2 * BLOCKS + n + 1),
                    "v": lambda: (v_ready, j * 2 * NT + 2 * n + 2),
                    "wo": lambda: (x1_ready, i * NT + n + 1),
                    "x2": lambda: (x2l_ready, i * NT + n + 1),
                    "gu": lambda: (inter_ready, i * 2 * NI + n + 1),
                    "dn": lambda: (y_ready, i * NT + n + 1),
                }[kind]()

            def dense(j, u, c):
                kind, n = u
                bank = dense_bank[u]
                at = order.index(u)
                if c == 0 and at >= 2:
                    wait(pe, *read_by(j, order[at - 2]))
                if kind == "xT":
                    if n == 0:
                        wait(pe, xn_ready, (j + 1) * NT)
                    for tt in range(NT):
                        i = nc.tensor.transpose(ps[:, bank, P * tt:P * tt + P], xa[:, tt, P * n:P * n + P], ident[:])
                    i.then_inc(xT_ps, 1)
                elif kind == "qk":
                    blk, k = divmod(n, 2)
                    if n == 0 and c == 0:
                        wait(pe, xT_act, 2 * j + 2)
                        wait(pe, xT_dve, 2 * j + 2)
                    i = mm(ps[:, bank, :], (wq_sb, wk_sb)[k][:, c, P * blk:P * blk + P], xT[:, c, :],
                           start=(c == 0), stop=(c == NC - 1))
                    if c == NC - 1:
                        i.then_inc(qk_ps, 1)
                elif kind == "v":
                    i = mm(ps[:, bank, :], xT[:, c, P * n:P * n + P], wv_sb[:, c, :], start=(c == 0), stop=(c == NC - 1))
                    if c == NC - 1:
                        i.then_inc(v_ps, 1)
                elif kind == "wo":
                    if n == 0 and c == 0:
                        wait(pe, aT_ready, j * BLOCKS)
                    i = mm(ps[:, bank, :], aT[:, c, P * n:P * n + P], wo_sb[:, c, :], start=(c == 0), stop=(c == NC - 1))
                    if c == NC - 1:
                        i.then_inc(wo_ps, 1)
                elif kind == "x2":
                    half, cc = divmod(n, 2)
                    if n == 0:
                        wait(pe, xn2_ready, j * NT)
                    for k in range(2):
                        for tt in range(2):
                            i = nc.tensor.transpose(ps[:, bank, HALF * k + P * tt:HALF * k + P * tt + P],
                                                    xa[:, 2 * half + tt, P * (2 * cc + k):P * (2 * cc + k) + P], ident[:])
                    i.then_inc(x2_ps, 1)
                elif kind == "gu":
                    half, ch = divmod(n, NI)
                    m = P if ch < NI - 1 else IR
                    if ch == 0 and c == 0:
                        wait(pe, x2l_ready, (j - 1) * NT + 2 * half + 2)
                    k, c0 = divmod(c, 2)
                    for cc in (2 * c0, 2 * c0 + 1):
                        for part in (x2h, x2l):
                            i = mm(ps[0:m, bank, HALF * k:HALF * k + HALF], (tg, tu)[k][:, cc, P * ch:P * ch + m],
                                   part[:, cc, :], start=(cc == 0 and part is x2h), stop=(cc == NC - 1 and part is x2l))
                    if c == NC - 1:
                        i.then_inc(gu_ps, 1)
                else:
                    half, tt = divmod(n, 2)
                    m = P if c < NI - 1 else IR
                    wait(pe, il_ready, (j - 1) * 2 * NI + NI * half + c + 1)
                    for part in (ih, il):
                        i = mm(ps[:, bank, :], part[0:m, c, P * tt:P * tt + P], td[0:m, c, :],
                               start=(c == 0 and part is ih), stop=(c == NI - 1 and part is il))
                    if c == NI - 1:
                        i.then_inc(dn_ps, 1)

            def max_fill(j, t, n):
                h, u = divmod(n, 3)
                s = t % SLOTS
                if n == 0:
                    wait(pe, stack_ready[s], 128 * (j * QUADS // SLOTS + t // SLOTS + 1))
                    wait(pe, max_ready, (j * QUADS + t) * MAXES)
                    wait(pe, mneg_ready, j * QUADS + t)
                elif n >= 2:
                    wait(pe, max_ready, (j * QUADS + t) * MAXES + READS[n - 2])
                for qb, at, k in (((3, 0, 512),), ((2, 0, 384),), ((1, 0, 256), (0, 256, 256)))[u]:
                    mm(ps[:, max_bank(t, n), at:at + k], qstk[s][0:MROW, h, P * qb:P * qb + P], kstk[s][0:MROW, h, 0:k],
                       start=True, stop=False)
                    i = mm(ps[:, max_bank(t, n), at + P * qb:at + P * qb + P], ident_b[:], future[:], start=False, stop=True)
                i.then_inc(max_ps, 1)

            def max_rows(j, t):
                wait(pe, max_ready, (j * QUADS + t + 1) * MAXES)
                for qb in range(NT):
                    i = nc.tensor.transpose(ps[0:QH, m_bank(t), P * qb:P * qb + P], mx[t % 2][:, qb, :], ident[:])
                i.then_inc(m_ps, 1)

            def fill(j, t, n):
                h, f = divmod(n, 3)
                wait(pe, exp_done, (j * QUADS + t) * FILLS + n - 1)
                s = t % SLOTS
                if n == 0:
                    wait(pe, mrow_ready, 16 * (j * QUADS + t + 1))
                q, k = qstk[s][0:MROW + 1, h, :], kstk[s][0:MROW + 1, h, :]
                for kb, q0, at in (((0, 0, 0),), ((1, 128, 0),), ((3, 256, 0), (2, 256, 256)))[f]:
                    i = mm(ps[:, SCORE_BANK + n % 2, at:at + L - q0], k[:, P * kb:P * kb + P], q[:, q0:L], start=True, stop=True)
                i.then_inc(scores_ready, 1)

            def weighted_sums(j, t):
                blk, e = divmod(t, 2)
                wait(pe, probs_masked, (j * QUADS + t + 1) * FILLS)
                if t == 0:
                    wait(pe, v_ready, (j + 1) * 2 * NT)
                if e == 0:
                    wait(pe, parts_joined, (j * BLOCKS + blk) * 2)
                for n, kb in enumerate((0, 1, 3, 2)):
                    at, q0 = SEG[kb]
                    for h in range(QH):
                        i = mm(ps[32 * h:32 * h + 32, SUM_BANK + e, q0:L], v_aug[:, kb, QH * blk + h, 32 * e:32 * e + 32],
                               probs[:, h, at:at + L - q0], start=(n == 0), stop=(n == NT - 1))
                i.then_inc(sums_done, 1)

            def iteration(j, attn, ffn):
                first = isinstance(j, int) and attn
                for u in BEFORE if attn else ():
                    if first and u == ("v", 0):
                        pe.wait_ge(wv_loaded, 16)
                    for c in range(1 if u[0] == "xT" else NC):
                        dense(j, u, c)
                for tt in range(NT):
                    if ffn:
                        for c in range(NC):
                            dense(j, ("wo", tt), c)
                    if attn:
                        for n in range(3 * tt, 3 * tt + 3):
                            max_fill(j, 0, n)
                if attn:
                    max_rows(j, 0)
                for t in range(QUADS):
                    pieces = placed(t, attn, ffn)
                    for pos in range(POS):
                        if attn and pos in FILL_AT:
                            fill(j, t, FILL_AT[pos])
                        if attn and pos in MAX_AT and t + 1 < QUADS:
                            max_fill(j, t + 1, MAX_AT[pos])
                        for u, c in pieces[pos]:
                            dense(j, u, c)
                        if attn and pos == M_AT and t + 1 < QUADS:
                            max_rows(j, t + 1)
                        if attn and pos == SUM_AT:
                            weighted_sums(j, t)
                    if first and t == max(SUM_STEPS):
                        pe.wait_ge(raw_summed, len(RAW))
                        pe.wait_ge(max_ready, (t + 2) * MAXES)
                        pe.wait_ge(mneg_ready, t + 2)
                        mm(ps[:, MAX_BANK + 1, 0:len(RAW)], ones[:], absum[:], start=True, stop=True).then_inc(sums_ready, 1)
                        pe.wait_ge(thr_step, 3)
                if first:
                    pe.wait_ge(wo_loaded, 16)
                    pe.wait_ge(ternary, len(RAW))

            pe.wait_ge(wqk_loaded, 32)
            pe.wait_ge(const_ready, CONSTS)
            dense_bank, order = banks(True, False), dense_order(True, False)
            iteration(0, True, False)
            dense_bank, order = banks(True, True), dense_order(True, True)
            with pe.Fori(1, B) as j:
                iteration(j, True, True)
            dense_bank, order = banks(False, True), dense_order(False, True)
            iteration(B, False, True)


def banks(attn, ffn):
    return {u: DENSE_BANK + n % 2 for n, u in enumerate(dense_order(attn, ffn))}


def max_bank(t, n):
    return MAX_BANK + (t * (FILLS + 1) + n) % 2


def m_bank(t):
    return max_bank(t, FILLS)


READS = [sum(2 if k % 3 == 2 else 1 for k in range(n + 1)) for n in range(FILLS)]
THR_STEPS = 8
CONSTS = 1 + 8 + 2 * (P // 32) + 1 + 3 * SLOTS + 1
_INS = ["x", "wq", "bq", "wk", "bk", "wv", "bv", "wo", "bo", "wg", "wu", "wd"]


def kernel(L0_attn_x, L0_attn_Wq, L0_attn_bq, L0_attn_Wk, L0_attn_bk, L0_attn_Wv, L0_attn_bv, L0_attn_Wo, L0_attn_bo,
           L0_ffn_w_gate, L0_ffn_w_up, L0_ffn_w_down):
    import numpy as np
    import concourse.bacc as bacc
    from concourse.bass_utils import run_bass_kernel_spmd

    def rows(w):
        w = np.asarray(w)
        r = w.reshape((BLOCKS, QH, 2, HD) + w.shape[1:])
        return np.ascontiguousarray(np.moveaxis(r, (2, 3, 1), (1, 2, 3)).reshape(w.shape))

    t = lambda w: np.ascontiguousarray(np.asarray(w).T)
    arrays = {
        "x": np.asarray(L0_attn_x), "wq": t(rows(L0_attn_Wq)), "bq": t(rows(L0_attn_bq).reshape(BLOCKS, P)), "wk": t(rows(L0_attn_Wk)),
        "bk": t(rows(L0_attn_bk).reshape(BLOCKS, P)), "wv": t(L0_attn_Wv), "bv": np.asarray(L0_attn_bv), "wo": t(L0_attn_Wo),
        "bo": np.asarray(L0_attn_bo), "wg": t(L0_ffn_w_gate), "wu": t(L0_ffn_w_up), "wd": t(L0_ffn_w_down),
    }
    nc = bacc.Bacc("TRN2", target_bir_lowering=False, num_devices=1)
    aps = [nc.dram_tensor(f"in_{n}", arrays[n].shape, mybir.dt.from_np(arrays[n].dtype), kind="ExternalInput").ap() for n in _INS]
    out = nc.dram_tensor("out", (B, L, D), F32, kind="ExternalOutput").ap()
    preln_block(nc, *aps, out)
    r = run_bass_kernel_spmd(nc, [{f"in_{n}": arrays[n] for n in _INS}], core_ids=[0])
    return r.results[0]["out"]
```

```python
import concourse.bass as bass
from concourse import mybir
from contextlib import ExitStack

F32 = mybir.dt.float32
F32R = mybir.dt.float32r
F16 = mybir.dt.float16
BF16 = mybir.dt.bfloat16
ALU = mybir.AluOpType
ACT = mybir.ActivationFunctionType
AX = mybir.AxisListType

P = 128
B, L, D = 4, 512, 512
H = 32
HD = D // H
I = 1376
NT = L // P
NC = D // P
NI = -(-I // P)
IR = I - (NI - 1) * P
HALF = L // 2
BLOCKS = D // P
QH = 4
QUADS = H // QH
SLOTS = 2
EPS = 1e-5
X2_SCALE = 64.0
INTER_SCALE = 2.0 ** -15
OUT_SCALE = 1.0 / (X2_SCALE * X2_SCALE * INTER_SCALE)
NEG = -1e30
MROW = P - 1
USED = 4 * HD

SEG = {0: (0, 0), 1: (512, 128), 3: (896, 384), 2: (1024, 256)}
PW = 1280
FILLS = 3 * QH
MAXES = 4 * QH
MAX_ORDER = [("fill", n) for n in range(FILLS)] + [("row", 0)]
READS = [sum(2 if k % 3 == 2 else 1 for k in range(n + 1)) for n in range(FILLS)]

MAX_BANK, DENSE_BANK, SCORE_BANK, SUM_BANK = 0, 2, 4, 6

POS = 20
FILL_AT = {n: n for n in range(FILLS)}
MAX_AT = {n + 2: n for n in range(FILLS)}
ROW_AT = 15
SUM_AT, LAST_SUM_AT = 17, 14
EVEN_AT = 2
JOIN_AT = {3: ("den",), 5: ("num",), 8: ("move",), 14: (0, 1), 15: (2,), 16: (3,)}
JOIN = ("den", "num", "move", 0, 1, 2, 3)
DIVIDE_AT = 17
STEPS = [
    [("qk", 2), ("x2", 0), ("x2", 1), ("qk", 3), ("gu", 0), ("gu", 1)],
    [("gu", n) for n in range(2, 8)],
    [("qk", 4), ("qk", 5)] + [("gu", n) for n in range(8, 10)],
    [("gu", 10), ("x2", 2), ("x2", 3), ("dn", 0), ("dn", 1)],
    [("qk", 6), ("qk", 7)] + [("gu", n) for n in range(11, 12)],
    [("gu", n) for n in range(12, 17)],
    [("gu", n) for n in range(17, 22)],
    [("dn", 2), ("dn", 3)],
]
ALONE = {0: (0, [("qk", 2), ("qk", 3)]), 1: (16, [("qk", 4)]), 2: (0, [("qk", 5)]), 3: (16, [("qk", 6)]),
         4: (0, [("qk", 7)])}
PIECES = {"xT": 1, "v": NC, "wo": NC, "qk": NC, "x2": 1, "gu": NC, "dn": NI}
FFN_KINDS = ("wo", "x2", "gu", "dn")
BEFORE = [("xT", n) for n in range(NC)] + [("qk", 0), ("qk", 1)] + [("v", n) for n in range(NT)]


def has(kind, attn, ffn):
    return ffn if kind in FFN_KINDS else attn


def dense_order(attn, ffn):
    order = BEFORE + [("wo", n) for n in range(NT)] + sum(STEPS, [])
    return [u for u in order if has(u[0], attn, ffn)]


def placed(t, attn, ffn):
    at = [[] for _ in range(POS)]
    if ffn:
        pieces = [(u, c) for u in STEPS[t] if has(u[0], attn, ffn) for c in range(PIECES[u[0]])]
        for n, piece in enumerate(pieces):
            at[n * POS // len(pieces)].append(piece)
    elif t in ALONE:
        first, units = ALONE[t]
        for n, piece in enumerate((u, c) for u in units for c in range(PIECES[u[0]])):
            at[first + n].append(piece)
    return at


def finished(t, attn, ffn, lag=0):
    at = [[] for _ in range(QUADS * POS)]
    for step in range(QUADS):
        for pos, pieces in enumerate(placed(step, attn, ffn)):
            at[min(step * POS + pos + lag, len(at) - 1)] += [u for u, c in pieces if c == PIECES[u[0]] - 1]
    return at[t * POS:t * POS + POS]


def start(attn, ffn):
    pieces = [(u, c) for u in BEFORE[-NT:] + [("wo", n) for n in range(NT)] if has(u[0], attn, ffn) for c in range(NC)]
    every = 2 if ffn else 1
    seq, todo = [], list(MAX_ORDER) if attn else []
    for n, (u, c) in enumerate(pieces):
        seq.append((u[0], u[1], c))
        if n >= NC and (n - NC) % every == every - 1 and todo:
            seq.append(todo.pop(0) + (0,))
    seq += [item + (0,) for item in todo]
    return seq


RAW = ([(0, c, 1, P, I) for c in range(NC)] + [(1, c, 1, P, I) for c in range(NC)]
       + [(2, c, 2, P, D) for c in range(0, NI - 1, 2)] + [(2, NI - 1, 1, IR, D)])
RAW_RING = 3
SUMS = (range(0, 3), range(3, 4), range(4, len(RAW)))
TERNARY = {0: range(0, 2), 1: range(2, 5), 2: range(5, 6), 3: range(6, 7), 4: range(7, 8), 5: range(8, 11),
           6: range(11, 12), 7: range(12, 14)}
POOL_TERNARY_AT, DVE_TERNARY_AT = (1, 5, 12), (15, 17, 19)


def raw_at(table, places, t, pos):
    return [n for n, at in zip(table.get(t, ()), places) if at == pos]


def preln_block(nc, x, wq, bq, wk, bk, wv, bv, wo, bo, wg, wu, wd, out):
    ctx = ExitStack()
    with ctx:
        def sb(name, shape, dt, where=ctx):
            return where.enter_context(nc.sbuf_tensor(name, shape, dt))

        def sem(name):
            return ctx.enter_context(nc.semaphore(name))

        wq_sb = sb("wq_sb", [P, NC, D], F32)
        wk_sb = sb("wk_sb", [P, NC, D], F32)
        wv_sb = sb("wv_sb", [P, NC, D], F32)
        wo_sb = sb("wo_sb", [P, NC, D], F32)
        tg = sb("tg", [P, NC, I], F16)
        tu = sb("tu", [P, NC, I], F16)
        td = sb("td", [P, NI, D], F16)
        bq_sb = sb("bq_sb", [P, BLOCKS], F32)
        bk_sb = sb("bk_sb", [P, BLOCKS], F32)
        bv_sb = sb("bv_sb", [P, D], F32)
        bo_sb = sb("bo_sb", [P, D], F32)
        ident = sb("ident", [P, P], F32)
        ident_b = sb("ident_b", [P, P], BF16)
        future = sb("future", [P, P], BF16)
        ones = sb("ones", [P, P], F32)
        is_even = sb("is_even", [P, 1], F32)
        is_odd = sb("is_odd", [P, 1], F32)
        minus_half = sb("minus_half", [P, NT], F32)
        scratch = sb("scratch", [P, NT], F32)
        absum = sb("absum", [P, len(RAW)], F32)
        wscale = sb("wscale", [P, 3], F32)
        wthr = sb("wthr", [P, 3], F32)
        wnthr = sb("wnthr", [P, 3], F32)
        fscale = sb("fscale", [P, 2], F32)
        xa = sb("xa", [P, NT, D], F32)
        xr = sb("xr", [P, NT, D], F32)
        stats = sb("stats", [P, NT, 6], F32)
        mv = sb("mv", [P, NT, 2], F32)
        rstd = sb("rstd", [P, NT, 1], F32)
        xT = sb("xT", [P, NC, L], F32)
        v_aug = sb("v_aug", [P, NT, H // 2, 64], F32)
        qstk = [sb(f"qstk{s}", [P, QH, L], F32R) for s in range(SLOTS)]
        kstk = [sb(f"kstk{s}", [P, QH, L], F32R) for s in range(SLOTS)]
        qk_hi = [sb(f"{n}_hi", [P, L], F32R) for n in "qk"]
        qk_lo = [sb(f"{n}_lo", [P, L], F32R) for n in "qk"]
        mx = [sb(f"mx{s}", [P, QH, NT], F32) for s in range(2)]
        mneg = sb("mneg", [QH * NT, P], F32R)
        probs = sb("probs", [P, QH, PW], F32)
        num = sb("num", [P, L], F32)
        den = sb("den", [P, L], F32)
        aT = sb("aT", [P, BLOCKS, L], F32)
        early = ExitStack()
        raw = [sb(f"raw{s}", [P, I], F32, early) for s in range(RAW_RING)]
        early.close()
        x2h = sb("x2h", [P, NC, HALF], F16)
        x2l = sb("x2l", [P, NC, HALF], F16)
        gate_s = [sb(f"gate_s{s}", [P, HALF], F32) for s in range(2)]
        inter = [sb(f"inter{s}", [P, HALF], F32) for s in range(2)]
        ih = sb("ih", [P, NI, HALF], F16)
        il = sb("il", [P, NI, HALF], F16)

        ps = ctx.enter_context(nc.psum_tensor("ps", [P, 8, 512], F32))

        x0_loaded = [sem(f"x0_loaded{t}") for t in range(NT)]
        xa_loaded = sem("xa_loaded")
        xr_loaded = sem("xr_loaded")
        wqk0_loaded = sem("wqk0_loaded")
        wqk_loaded = sem("wqk_loaded")
        wv_loaded = sem("wv_loaded")
        wo_loaded = sem("wo_loaded")
        bias_loaded = sem("bias_loaded")
        raw_loaded = [sem(f"raw_loaded{s}") for s in range(RAW_RING)]
        const_ready = sem("const_ready")
        table_loaded = sem("table_loaded")
        raw_summed = sem("raw_summed")
        sums_ready = sem("sums_ready")
        thr_step = sem("thr_step")
        negatives = sem("negatives")
        ternary = sem("ternary")
        stats_ready = sem("stats_ready")
        mv_ready = sem("mv_ready")
        rstd_step = sem("rstd_step")
        rstd_ready = sem("rstd_ready")
        xn_ready = sem("xn_ready")
        xn2_ready = sem("xn2_ready")
        xT_ps = sem("xT_ps")
        xT_act = sem("xT_act")
        xT_dve = sem("xT_dve")
        qk_ps = sem("qk_ps")
        hi_ready = sem("hi_ready")
        lo_ready = sem("lo_ready")
        stack_ready = [sem(f"stack_ready{s}") for s in range(SLOTS)]
        v_ps = sem("v_ps")
        v_ready = sem("v_ready")
        max_ps = sem("max_ps")
        max_ready = sem("max_ready")
        m_ps = sem("m_ps")
        mneg_ready = sem("mneg_ready")
        mrow_ready = sem("mrow_ready")
        scores_ready = sem("scores_ready")
        exp_done = sem("exp_done")
        probs_masked = sem("probs_masked")
        sums_done = sem("sums_done")
        even_parts = sem("even_parts")
        parts_joined = sem("parts_joined")
        den_moved = sem("den_moved")
        rden_ready = sem("rden_ready")
        aT_ready = sem("aT_ready")
        xbo_ready = sem("xbo_ready")
        wo_ps = sem("wo_ps")
        x1_ready = sem("x1_ready")
        x2_ps = sem("x2_ps")
        x2h_ready = sem("x2h_ready")
        x2l_ready = sem("x2l_ready")
        gu_ps = sem("gu_ps")
        gate_ready = sem("gate_ready")
        inter_ready = sem("inter_ready")
        ih_ready = sem("ih_ready")
        il_ready = sem("il_ready")
        dn_ps = sem("dn_ps")
        y_ready = sem("y_ready")
        stored = sem("stored")
        pool_alone = sem("pool_alone")
        dve_alone = sem("dve_alone")
        sp_alone = sem("sp_alone")

        x_v = x.rearrange("b (t p) d -> b p t d", p=P)
        out_v = out.rearrange("b (t p) d -> b p t d", p=P)

        def wait(eng, s, value, carrier=None):
            if isinstance(value, int) and value <= 0:
                return
            eng.wait_ge(s, value)
            if carrier is not None:
                eng.sem_inc(carrier, 1)

        def load_raw(eng, n):
            m, c, k, rows, cols = RAW[n % len(RAW)]
            wait(eng, raw_summed, min(n - RAW_RING + 1, len(RAW)))
            wait(eng, ternary, n - RAW_RING + 1 - len(RAW))
            src = (wg, wu, wd)[m]
            src = src[P * c:P * (c + k - 1) + rows, :].rearrange("(k p) n -> p k n", p=rows)
            eng.dma_start(raw[n % RAW_RING][0:rows, 0:k * cols].rearrange("p (k n) -> p k n", k=k), src)\
               .then_inc(raw_loaded[n % RAW_RING], 16)

        block = ctx.enter_context(nc.Block())

        @block.sync
        def _(sp):
            for tt in range(NT):
                sp.dma_start(xa[:, tt, :], x_v[0, :, tt]).then_inc(x0_loaded[tt], 16)
            def load_qk(lo, hi, s):
                for dst, src in ((wq_sb, wq), (wk_sb, wk)):
                    sp.dma_start(dst[:, :, lo:hi], src.rearrange("(c p) n -> p c n", p=P)[:, :, lo:hi]).then_inc(s, 16)

            load_qk(0, P, wqk0_loaded)
            sp.dma_start(wv_sb[:], wv.rearrange("(c p) n -> p c n", p=P)).then_inc(wv_loaded, 16)
            for n in range(RAW_RING):
                load_raw(sp, n)
            def stack(j, t):
                s, blk, e = t % SLOTS, t // 2, t % 2
                wait(sp, scores_ready, (j * QUADS + t - SLOTS + 1) * FILLS, sp_alone)
                for k, stk in enumerate((qstk, kstk)):
                    wait(sp, lo_ready, j * 2 * BLOCKS + 2 * blk + k + 1, sp_alone)
                    for n in range(4):
                        part = (qk_hi, qk_lo)[n % 2 if k == 0 else n // 2][k]
                        sp.dma_start(stk[s][HD * n:HD * n + HD, :, :].bitcast(F32),
                                     part[64 * e:64 * e + 64, :].bitcast(F32)).then_inc(stack_ready[s], 16)

            def iteration(j, attn, ffn):
                first = isinstance(j, int) and attn
                if attn:
                    stack(j, 0)
                    stack(j, 1)
                if first:
                    load_qk(P, D, wqk_loaded)
                for t in range(QUADS):
                    if attn and t + 2 < QUADS:
                        stack(j, t + 2)
                    if first and t == 2:
                        sp.dma_start(xr[:], x_v[0]).then_inc(xr_loaded, 16)
                        sp.dma_start(wo_sb[:], wo.rearrange("(c p) n -> p c n", p=P)).then_inc(wo_loaded, 16)
                    for n in TERNARY.get(t, ()) if first else ():
                        if n + RAW_RING < len(RAW):
                            load_raw(sp, len(RAW) + n + RAW_RING)
                    if attn and t == 4:
                        if ffn:
                            wait(sp, x2_ps, (j - 1) * NT + NT, sp_alone)
                            sp.dma_start(xa[:], x_v[(j + 1) % B]).then_inc(xa_loaded, 16)
                        else:
                            wait(sp, xT_ps, NC)
                            sp.dma_start(xa[:], x_v[1]).then_inc(xa_loaded, 16)
                if ffn:
                    wait(sp, y_ready, j * NT + 2, sp_alone)
                    sp.dma_start(out_v[j - 1], xr[:]).then_inc(stored, 16)
                    wait(sp, stored, 16 * j, sp_alone)
                    if attn:
                        sp.dma_start(xr[:], x_v[j]).then_inc(xr_loaded, 16)

            iteration(0, True, False)
            with sp.Fori(1, B) as j:
                iteration(j, True, True)
            iteration(B, False, True)

        @block.gpsimd
        def _(g):
            pool = nc.gpsimd
            for src, dst in ((bq, bq_sb), (bk, bk_sb)):
                g.dma_start(dst[:], src).then_inc(bias_loaded, 16)
            for src, dst in ((bv, bv_sb), (bo, bo_sb)):
                g.dma_start(dst[:], src.partition_broadcast(P)).then_inc(bias_loaded, 16)
            n_const = 0

            def step(i):
                nonlocal n_const
                n_const += 1
                i.then_inc(const_ready, 1)
                g.wait_ge(const_ready, n_const)
            step(pool.memset(minus_half[:], -0.5))

            def rsqrt(count, scale):
                wait(g, mv_ready, count * NT, pool_alone)
                pool.tensor_scalar(rstd[:, :, 0], mv[:, :, 1], EPS, scale ** -2, ALU.add, ALU.mult).then_inc(rstd_step, 1)
                g.wait_ge(rstd_step, count)
                pool.tensor_tensor(rstd[:, :, 0], rstd[:, :, 0], minus_half[:], ALU.pow).then_inc(rstd_ready, 1)

            step(pool.memset(ident[:], 0.0))
            step(pool.affine_select(out=ident[:], in_=ident[:], compare_op=ALU.not_equal, fill=1.0,
                                    base=0, pattern=[[-1, P]], channel_multiplier=1))
            step(pool.memset(absum[:], 0.0))
            assert n_const == FIRST_CONSTS
            rsqrt(1, 1.0)
            step(pool.tensor_copy(ident_b[:], ident[:]))
            step(pool.memset(ones[:], 0.0))
            step(pool.affine_select(out=future[:], in_=ones[:], compare_op=ALU.is_ge, fill=NEG,
                                    base=0, pattern=[[-1, P]], channel_multiplier=1))
            step(pool.memset(ones[:], 1.0))
            step(pool.memset(is_odd[:], 0.0))
            for k in range(P // 32):
                step(pool.affine_select(out=is_odd[:], in_=is_odd[:], compare_op=ALU.is_gt, fill=1.0,
                                        base=32 * k + 16, pattern=[[0, 1]], channel_multiplier=-1))
                step(pool.affine_select(out=is_odd[:], in_=is_odd[:], compare_op=ALU.is_gt, fill=0.0,
                                        base=32 * k + 32, pattern=[[0, 1]], channel_multiplier=-1))
            step(pool.tensor_scalar(is_even[:], is_odd[:], -1.0, 1.0, ALU.mult, ALU.add))
            for s in range(SLOTS):
                for stk, fixed in ((qstk, 0.0), (kstk, 1.0)):
                    step(pool.memset(stk[s][USED:P, :, :].bitcast(F32), fixed))
            step(pool.memset(v_aug[:, :, :, HD:HD + 32], 1.0))
            assert n_const == CONSTS
            g.wait_ge(bias_loaded, 64)

            def mask(j, t, n):
                h, f = divmod(n, 3)
                wait(g, exp_done, (j * QUADS + t) * FILLS + n + 1, pool_alone)
                at = SEG[(0, 1, 3)[f]][0]
                k = (1, 1, 2)[f]
                v = probs[:, h, at:at + k * P].rearrange("p (a q) -> p a q", a=k)
                pool.affine_select(out=v, in_=v, compare_op=ALU.is_ge, fill=0.0, base=0,
                                   pattern=[[0, k], [1, P]], channel_multiplier=-1).then_inc(probs_masked, 1)

            def divide(j, blk):
                if blk == 0:
                    wait(g, wo_ps, j * NT)
                for tt in range(NT):
                    wait(g, rden_ready, (j * BLOCKS + blk) * NT + tt + 1)
                    part = slice(P * tt, P * tt + P)
                    pool.tensor_tensor(aT[:, blk, part], num[:, part], den[:, part], ALU.mult).then_inc(aT_ready, 1)

            def parts(i, n):
                half, ch = divmod(n, NI)
                m = P if ch < NI - 1 else IR
                wait(g, inter_ready, i * 2 * NI + n + 1)
                g.sem_inc(pool_alone, 1)
                pool.tensor_copy(ih[0:m, ch, :], inter[n % 2][0:m, :]).then_inc(ih_ready, 1)
                wait(g, ih_ready, i * 2 * NI + n + 1)
                pool.tensor_tensor(il[0:m, ch, :], inter[n % 2][0:m, :], ih[0:m, ch, :], ALU.subtract).then_inc(il_ready, 1)

            def iteration(j, attn, ffn):
                first = isinstance(j, int) and attn
                if ffn:
                    divide(j - 1, BLOCKS - 1)
                    wait(g, xr_loaded, 16 * j)
                    for tt in range(NT):
                        pool.tensor_tensor(xr[:, tt, :], xr[:, tt, :], bo_sb[:], ALU.add).then_inc(xbo_ready, 1)
                    rsqrt(2 * j + 1, X2_SCALE)
                for t in range(QUADS):
                    done = finished(t, attn, ffn, 2)
                    for pos in range(POS):
                        if attn and pos in FILL_AT:
                            mask(j, t, FILL_AT[pos])
                        for kind, n in done[pos]:
                            if kind == "gu":
                                parts(j - 1, n)
                        if attn and pos == DIVIDE_AT and t % 2 == 0 and t:
                            divide(j, t // 2 - 1)
                        for n in raw_at(TERNARY, POOL_TERNARY_AT, t, pos) if first else ():
                            m, c, k, rows, cols = RAW[n]
                            l = n + len(RAW)
                            wait(g, raw_loaded[l % RAW_RING], 16 * (l // RAW_RING + 1))
                            wait(g, thr_step, THR_STEPS)
                            pool.tensor_scalar((tg, tu, td)[m][0:rows, c:c + k, :],
                                               raw[l % RAW_RING][0:rows, 0:k * cols].rearrange("p (k n) -> p k n", k=k),
                                               wnthr[0:rows, m:m + 1], None, ALU.is_lt).then_inc(negatives, 1)
                    if attn and t == 6:
                        rsqrt(2 * j + 2, 1.0)

            iteration(0, True, False)
            with g.Fori(1, B) as j:
                iteration(j, True, True)
            iteration(B, False, True)

        @block.scalar
        def _(a):
            act = nc.scalar

            def high_part(j, n):
                blk, k = divmod(n, 2)
                wait(a, qk_ps, j * 2 * BLOCKS + n + 1)
                for s in range(SLOTS):
                    wait(a, stack_ready[s], 128 * (j * QUADS // SLOTS + blk))
                act.activation(qk_hi[k][:], ps[:, dense_bank["qk", n], :], ACT.Identity,
                               bias=(bq_sb, bk_sb)[k][:, blk:blk + 1]).then_inc(hi_ready, 1)

            def max_row(j, t):
                wait(a, m_ps, j * QUADS + t + 1)
                wait(a, mrow_ready, 16 * (j * QUADS + t))
                act.activation(mneg[:], ps[0:QH * NT, max_bank(t, "row", 0), 0:P], ACT.Copy, scale=-1.0).then_inc(mneg_ready, 1)
                wait(a, mneg_ready, j * QUADS + t + 1)
                a.dma_start(qstk[t % SLOTS][MROW:MROW + 1, :, :].bitcast(F32), mneg[:].bitcast(F32)).then_inc(mrow_ready, 16)

            def exps(j, t, n):
                h, f = divmod(n, 3)
                wait(a, scores_ready, (j * QUADS + t) * FILLS + n + 1)
                if n < 3:
                    wait(a, sums_done, (j * QUADS + t - 1) * NT + (1, 2, 4)[n])
                lo, hi = ((0, 512), (0, 384), (128, 512))[f]
                at = SEG[(0, 1, 3)[f]][0]
                act.activation(probs[:, h, at:at + hi - lo], ps[:, SCORE_BANK + n % 2, lo:hi], ACT.Exp,
                               scale=HD ** -0.5).then_inc(exp_done, 1)

            def even_heads(j, blk):
                wait(a, sums_done, (j * QUADS + 2 * blk + 2) * NT)
                wait(a, aT_ready, (j * BLOCKS + blk) * NT)
                act.activation(num[:], ps[:, SUM_BANK, :], ACT.Copy, scale=is_even[:]).then_inc(even_parts, 1)
                act.activation(den[:], ps[:, SUM_BANK, :], ACT.Copy, scale=is_odd[:]).then_inc(even_parts, 1)

            def gate(i, n):
                m = P if n % NI < NI - 1 else IR
                wait(a, gu_ps, i * 2 * NI + n + 1)
                if n >= 2:
                    wait(a, inter_ready, i * 2 * NI + n - 1)
                act.activation(gate_s[n % 2][0:m, :], ps[0:m, dense_bank["gu", n], 0:HALF], ACT.Copy,
                               scale=INTER_SCALE).then_inc(gate_ready, 1)

            def magnitudes(n):
                m, c, k, rows, cols = RAW[n]
                a.wait_ge(raw_loaded[n % RAW_RING], 16 * (n // RAW_RING + 1))
                act.activation((tg, tu, td)[m][0:rows, c:c + k, :],
                               raw[n % RAW_RING][0:rows, 0:k * cols].rearrange("p (k n) -> p k n", k=k),
                               ACT.Abs, accum_out=absum[0:rows, n:n + 1]).then_inc(raw_summed, 1)
                load_raw(a, n + RAW_RING)

            def x2_high(i, n):
                wait(a, x2_ps, i * NT + n + 1)
                c = 2 * (n % 2)
                act.activation(x2h[:, c:c + 2, :], ps[:, dense_bank["x2", n], :].rearrange("p (c t) -> p c t", c=2),
                               ACT.Copy).then_inc(x2h_ready, 1)

            def iteration(j, attn, ffn):
                first = isinstance(j, int) and attn
                if attn:
                    for c in (0, 1):
                        wait(a, xT_ps, j * NC + c + 1)
                        act.activation(xT[:, c, :], ps[:, dense_bank["xT", c], :], ACT.Copy).then_inc(xT_act, 1)
                    for k in range(2):
                        for n in SUMS[k] if first else ():
                            magnitudes(n)
                        if first:
                            a.wait_ge(bias_loaded, 64)
                        high_part(j, k)
                if first:
                    for n in SUMS[2]:
                        magnitudes(n)
                    a.wait_ge(const_ready, CONSTS)
                if ffn:
                    even_heads(j - 1, BLOCKS - 1)
                if attn:
                    max_row(j, 0)
                for t in range(QUADS):
                    done = finished(t, attn, ffn)
                    for pos in range(POS):
                        if attn and pos in FILL_AT:
                            exps(j, t, FILL_AT[pos])
                        for kind, n in done[pos]:
                            if kind == "qk":
                                high_part(j, n)
                            elif kind == "x2":
                                x2_high(j - 1, n)
                            elif kind == "gu":
                                gate(j - 1, n)
                        if attn and pos == EVEN_AT and t % 2 == 0 and t:
                            even_heads(j, t // 2 - 1)
                        if attn and pos == ROW_AT and t + 1 < QUADS:
                            max_row(j, t + 1)
            a.wait_ge(const_ready, FIRST_CONSTS)
            act.activation(scratch[:], minus_half[:], ACT.Exp).then_inc(table_loaded, 1)
            dense_bank = banks(True, False)
            iteration(0, True, False)
            dense_bank = banks(True, True)
            with a.Fori(1, B) as j:
                iteration(j, True, True)
            dense_bank = banks(False, True)
            iteration(B, False, True)

        @block.vector
        def _(v):
            dve = nc.vector

            def moments(count):
                for tt in range(NT):
                    wait(v, stats_ready, (count - 1) * NT + tt + 1, dve_alone)
                    dve.bn_aggr(mv[:, tt, :], stats[:, tt, :]).then_inc(mv_ready, 1)

            def normalise(count, src, dst, ready):
                wait(v, rstd_ready, count)
                for tt in range(NT):
                    dve.tensor_scalar(dst[:, tt, :], src[:, tt, :], mv[:, tt, 0:1], rstd[:, tt, :],
                                      ALU.subtract, ALU.mult).then_inc(ready, 1)

            def low_part(j, n):
                blk, k = divmod(n, 2)
                wait(v, hi_ready, j * 2 * BLOCKS + n + 1)
                dve.scalar_tensor_tensor(out=qk_lo[k][:], in0=ps[:, dense_bank["qk", n], :],
                                         scalar=(bq_sb, bk_sb)[k][:, blk:blk + 1], in1=qk_hi[k][:].bitcast(F32),
                                         op0=ALU.add, op1=ALU.subtract).then_inc(lo_ready, 1)

            def maxima(j, t, n):
                h, u = divmod(n, 3)
                wait(v, max_ps, (j * QUADS + t) * FILLS + n + 1)
                for i, lo, hi in (((3, 0, 512),), ((2, 0, 384),), ((1, 0, 256), (0, 256, 384)))[u]:
                    dve.reduce_max(mx[t % 2][:, h, i:i + 1], ps[:, max_bank(t, "fill", n), lo:hi], AX.X).then_inc(max_ready, 1)

            def join(j, blk, pieces):
                for what in pieces:
                    if what == "den":
                        wait(v, even_parts, j * 2 * BLOCKS + 2 * blk + 2)
                        dve.scalar_tensor_tensor(out=den[:], in0=ps[:, SUM_BANK + 1, :], scalar=is_even[:], in1=den[:],
                                                 op0=ALU.mult, op1=ALU.add).then_inc(parts_joined, 1)
                    elif what == "num":
                        dve.scalar_tensor_tensor(out=num[:], in0=ps[:, SUM_BANK + 1, :], scalar=is_odd[:], in1=num[:],
                                                 op0=ALU.mult, op1=ALU.add).then_inc(parts_joined, 1)
                    elif what == "move":
                        wait(v, parts_joined, j * 2 * BLOCKS + 2 * blk + 2, dve_alone)
                        dve.stream_shuffle(den[:], den[:], [(i + HD) % 32 for i in range(32)]).then_inc(den_moved, 1)
                    else:
                        if what == 0:
                            wait(v, den_moved, j * BLOCKS + blk + 1)
                        part = den[:, P * what:P * what + P]
                        dve.reciprocal(part, part).then_inc(rden_ready, 1)

            def values(j, tt):
                wait(v, v_ps, j * NT + tt + 1)
                for e in range(2):
                    dve.tensor_tensor(v_aug[:, tt, :, 48 * e:48 * e + HD],
                                      ps[:, dense_bank["v", tt], :].rearrange("p (j e r) -> p j e r", e=2, r=HD)[:, :, e, :],
                                      bv_sb[:].rearrange("p (j e r) -> p j e r", e=2, r=HD)[:, :, e, :],
                                      ALU.add).then_inc(v_ready, 1)

            def residual(i, tt):
                wait(v, wo_ps, i * NT + tt + 1)
                wait(v, xbo_ready, i * NT + tt + 1)
                dve.tensor_tensor(xr[:, tt, :], ps[:, dense_bank["wo", tt], :], xr[:, tt, :], ALU.add).then_inc(x1_ready, 1)
                wait(v, x1_ready, i * NT + tt + 1)
                dve.bn_stats(stats[:, tt, :], xr[:, tt, :]).then_inc(stats_ready, 1)

            def product(i, n):
                m = P if n % NI < NI - 1 else IR
                wait(v, gate_ready, i * 2 * NI + n + 1)
                if n >= 2:
                    wait(v, il_ready, i * 2 * NI + n - 1)
                dve.tensor_tensor(inter[n % 2][0:m, :], ps[0:m, dense_bank["gu", n], HALF:], gate_s[n % 2][0:m, :],
                                  ALU.mult).then_inc(inter_ready, 1)

            def x2_low(i, n):
                wait(v, x2h_ready, i * NT + n + 1)
                c = 2 * (n % 2)
                dve.tensor_tensor(x2l[:, c:c + 2, :], ps[:, dense_bank["x2", n], :].rearrange("p (c t) -> p c t", c=2),
                                  x2h[:, c:c + 2, :], ALU.subtract).then_inc(x2l_ready, 1)

            def result(i, tt):
                wait(v, dn_ps, i * NT + tt + 1)
                dve.scalar_tensor_tensor(out=xr[:, tt, :], in0=ps[:, dense_bank["dn", tt], :], scalar=fscale[:, 1:2],
                                         in1=xr[:, tt, :], op0=ALU.mult, op1=ALU.add).then_inc(y_ready, 1)

            n_thr = 0

            def thr(i):
                nonlocal n_thr
                n_thr += 1
                i.then_inc(thr_step, 1)
                v.wait_ge(thr_step, n_thr)

            def thresholds():
                v.wait_ge(sums_ready, 1)
                a = 0
                for m in range(3):
                    k = sum(r[0] == m for r in RAW)
                    thr(dve.reduce_sum(wscale[:, m:m + 1], ps[:, MAX_BANK + 1, a:a + k], AX.X))
                    a += k
                thr(dve.tensor_scalar(wscale[:], wscale[:], 1.0 / (D * I), None, ALU.mult))
                thr(dve.tensor_scalar(wthr[:], wscale[:], EPS, 0.5, ALU.add, ALU.mult))
                thr(dve.tensor_scalar(wnthr[:], wthr[:], -1.0, None, ALU.mult))
                thr(dve.tensor_tensor(fscale[:, 0:1], wscale[:, 0:1], wscale[:, 1:2], ALU.mult))
                thr(dve.scalar_tensor_tensor(out=fscale[:, 1:2], in0=fscale[:, 0:1], scalar=OUT_SCALE,
                                             in1=wscale[:, 2:3], op0=ALU.mult, op1=ALU.mult))
                assert n_thr == THR_STEPS

            def make_ternary(n):
                m, c, k, rows, cols = RAW[n]
                l = n + len(RAW)
                t = (tg, tu, td)[m][0:rows, c:c + k, :]
                v.wait_ge(negatives, n + 1)
                dve.scalar_tensor_tensor(out=t, in0=raw[l % RAW_RING][0:rows, 0:k * cols].rearrange("p (k n) -> p k n", k=k),
                                         scalar=wthr[0:rows, m:m + 1], in1=t, op0=ALU.is_gt, op1=ALU.subtract).then_inc(ternary, 1)

            def iteration(j, attn, ffn):
                first = isinstance(j, int) and attn
                if attn:
                    for c in (2, 3):
                        wait(v, xT_ps, j * NC + c + 1)
                        dve.tensor_copy(xT[:, c, :], ps[:, dense_bank["xT", c], :]).then_inc(xT_dve, 1)
                    if first:
                        v.wait_ge(bias_loaded, 64)
                    low_part(j, 0)
                    low_part(j, 1)
                if first:
                    v.wait_ge(const_ready, CONSTS)
                if ffn:
                    join(j - 1, BLOCKS - 1, JOIN)
                for kind, n, c in start(attn, ffn):
                    if kind == "fill":
                        maxima(j, 0, n)
                    elif kind == "v" and c == NC - 1:
                        values(j, n)
                    elif kind == "wo" and c == NC - 1:
                        residual(j - 1, n)
                if first:
                    thresholds()
                if ffn:
                    moments(2 * j + 1)
                    normalise(2 * j + 1, xr, xa, xn2_ready)
                for t in range(QUADS):
                    done = finished(t, attn, ffn, 1)
                    if attn and t == QUADS - 1:
                        normalise(2 * j + 2, xa, xa, xn_ready)
                    for pos in range(POS):
                        if attn and pos in MAX_AT and t + 1 < QUADS:
                            maxima(j, t + 1, MAX_AT[pos])
                        for kind, n in done[pos]:
                            if kind == "qk":
                                low_part(j, n)
                            elif kind == "x2":
                                x2_low(j - 1, n)
                            elif kind == "gu":
                                product(j - 1, n)
                            elif kind == "dn":
                                result(j - 1, n)
                        if attn and pos in JOIN_AT and t % 2 == 0 and t:
                            join(j, t // 2 - 1, JOIN_AT[pos])
                        for n in raw_at(TERNARY, DVE_TERNARY_AT, t, pos) if first else ():
                            make_ternary(n)
                    if attn and t == 5:
                        wait(v, xa_loaded, 16 * (j + 1))
                        for tt in range(NT):
                            dve.bn_stats(stats[:, tt, :], xa[:, tt, :]).then_inc(stats_ready, 1)
                        moments(2 * j + 2)
                if first:
                    v.sem_inc(y_ready, 2)

            for tt in range(NT):
                v.wait_ge(x0_loaded[tt], 16)
                dve.bn_stats(stats[:, tt, :], xa[:, tt, :]).then_inc(stats_ready, 1)
            moments(1)
            normalise(1, xa, xa, xn_ready)
            dense_bank = banks(True, False)
            iteration(0, True, False)
            dense_bank = banks(True, True)
            with v.Fori(1, B) as j:
                iteration(j, True, True)
            dense_bank = banks(False, True)
            iteration(B, False, True)

        @block.tensor
        def _(pe):
            mm = nc.tensor.matmul

            def read_by(j, u):
                kind, n = u
                i = j - 1
                return {
                    "xT": lambda: (xT_act, j * 2 + n + 1) if n < 2 else (xT_dve, j * 2 + n - 1),
                    "qk": lambda: (lo_ready, j * 2 * BLOCKS + n + 1),
                    "v": lambda: (v_ready, j * 2 * NT + 2 * n + 2),
                    "wo": lambda: (x1_ready, i * NT + n + 1),
                    "x2": lambda: (x2l_ready, i * NT + n + 1),
                    "gu": lambda: (inter_ready, i * 2 * NI + n + 1),
                    "dn": lambda: (y_ready, i * NT + n + 3),
                }[kind]()

            def dense(j, u, c):
                kind, n = u
                bank = dense_bank[u]
                at = order.index(u)
                if c == 0:
                    if at >= 2:
                        wait(pe, *read_by(j, order[at - 2]))
                    else:
                        wait(pe, y_ready, (j - 1) * NT + at + 1)
                if kind == "xT":
                    if n == 0:
                        wait(pe, xn_ready, (j + 1) * NT)
                    for tt in range(NT):
                        i = nc.tensor.transpose(ps[:, bank, P * tt:P * tt + P], xa[:, tt, P * n:P * n + P], ident[:])
                    i.then_inc(xT_ps, 1)
                elif kind == "qk":
                    blk, k = divmod(n, 2)
                    if n == 0 and c == 0:
                        wait(pe, xT_act, 2 * j + 2)
                        wait(pe, xT_dve, 2 * j + 2)
                    i = mm(ps[:, bank, :], (wq_sb, wk_sb)[k][:, c, P * blk:P * blk + P], xT[:, c, :],
                           start=(c == 0), stop=(c == NC - 1))
                    if c == NC - 1:
                        i.then_inc(qk_ps, 1)
                elif kind == "v":
                    i = mm(ps[:, bank, :], xT[:, c, P * n:P * n + P], wv_sb[:, c, :], start=(c == 0), stop=(c == NC - 1))
                    if c == NC - 1:
                        i.then_inc(v_ps, 1)
                elif kind == "wo":
                    if c == 0:
                        wait(pe, aT_ready, (j * BLOCKS - 1) * NT + n + 1)
                    i = mm(ps[:, bank, :], aT[:, c, P * n:P * n + P], wo_sb[:, c, :], start=(c == 0), stop=(c == NC - 1))
                    if c == NC - 1:
                        i.then_inc(wo_ps, 1)
                elif kind == "x2":
                    half, cc = divmod(n, 2)
                    if cc == 0:
                        wait(pe, xn2_ready, (j - 1) * NT + 2 * half + 2)
                    for k in range(2):
                        for tt in range(2):
                            i = nc.tensor.transpose(ps[:, bank, HALF * k + P * tt:HALF * k + P * tt + P],
                                                    xa[:, 2 * half + tt, P * (2 * cc + k):P * (2 * cc + k) + P], ident[:])
                    i.then_inc(x2_ps, 1)
                elif kind == "gu":
                    half, ch = divmod(n, NI)
                    m = P if ch < NI - 1 else IR
                    if ch == 0 and c == 0:
                        wait(pe, x2l_ready, (j - 1) * NT + 2 * half + 2)
                    k, c0 = divmod(c, 2)
                    for cc in (2 * c0, 2 * c0 + 1):
                        for part in (x2h, x2l):
                            i = mm(ps[0:m, bank, HALF * k:HALF * k + HALF], (tg, tu)[k][:, cc, P * ch:P * ch + m],
                                   part[:, cc, :], start=(cc == 0 and part is x2h), stop=(cc == NC - 1 and part is x2l))
                    if c == NC - 1:
                        i.then_inc(gu_ps, 1)
                else:
                    half, tt = divmod(n, 2)
                    m = P if c < NI - 1 else IR
                    wait(pe, il_ready, (j - 1) * 2 * NI + NI * half + c + 1)
                    for part in (ih, il):
                        i = mm(ps[:, bank, :], part[0:m, c, P * tt:P * tt + P], td[0:m, c, :],
                               start=(c == 0 and part is ih), stop=(c == NI - 1 and part is il))
                    if c == NI - 1:
                        i.then_inc(dn_ps, 1)

            def max_bank_read(j, t, what, n):
                k = MAX_ORDER.index((what, n)) - 2
                last, m = MAX_ORDER[k]
                quads = j * QUADS + t - (1 if k < 0 else 0)
                if last == "fill":
                    return max_ready, quads * MAXES + READS[m]
                return mneg_ready, quads + 1

            def max_fill(j, t, n):
                h, u = divmod(n, 3)
                s = t % SLOTS
                bank = max_bank(t, "fill", n)
                if n == 0:
                    wait(pe, stack_ready[s], 128 * (j * QUADS // SLOTS + t // SLOTS + 1))
                wait(pe, *max_bank_read(j, t, "fill", n))
                for qb, at, k in (((3, 0, 512),), ((2, 0, 384),), ((1, 0, 256), (0, 256, 256)))[u]:
                    mm(ps[:, bank, at:at + k], qstk[s][0:MROW, h, P * qb:P * qb + P], kstk[s][0:MROW, h, 0:k],
                       start=True, stop=False)
                    i = mm(ps[:, bank, at + P * qb:at + P * qb + P], ident_b[:], future[:], start=False, stop=True)
                i.then_inc(max_ps, 1)

            def max_rows(j, t):
                wait(pe, *max_bank_read(j, t, "row", 0))
                wait(pe, max_ready, (j * QUADS + t + 1) * MAXES)
                nc.tensor.transpose(ps[0:QH * NT, max_bank(t, "row", 0), 0:P],
                                    mx[t % 2][:].rearrange("p h q -> p (h q)"), ident[:]).then_inc(m_ps, 1)

            def fill(j, t, n):
                h, f = divmod(n, 3)
                wait(pe, exp_done, (j * QUADS + t) * FILLS + n - 1)
                s = t % SLOTS
                if n == 0:
                    wait(pe, mrow_ready, 16 * (j * QUADS + t + 1))
                q, k = qstk[s][0:MROW + 1, h, :], kstk[s][0:MROW + 1, h, :]
                for kb, q0, at in (((0, 0, 0),), ((1, 128, 0),), ((3, 256, 0), (2, 256, 256)))[f]:
                    i = mm(ps[:, SCORE_BANK + n % 2, at:at + L - q0], k[:, P * kb:P * kb + P], q[:, q0:L], start=True, stop=True)
                i.then_inc(scores_ready, 1)

            def weighted_sums(j, t):
                blk, e = divmod(t, 2)
                wait(pe, probs_masked, (j * QUADS + t + 1) * FILLS)
                if t == 0:
                    wait(pe, v_ready, (j + 1) * 2 * NT)
                if e == 0:
                    wait(pe, parts_joined, (j * BLOCKS + blk) * 2)
                for n, kb in enumerate((0, 1, 3, 2)):
                    at, q0 = SEG[kb]
                    for h in range(QH):
                        i = mm(ps[32 * h:32 * h + 32, SUM_BANK + e, q0:L], v_aug[:, kb, QH * blk + h, 32 * e:32 * e + 32],
                               probs[:, h, at:at + L - q0], start=(n == 0), stop=(n == NT - 1))
                    i.then_inc(sums_done, 1)

            def iteration(j, attn, ffn):
                first = isinstance(j, int) and attn
                for u in BEFORE[:-NT] if attn else ():
                    for c in range(PIECES[u[0]]):
                        dense(j, u, c)
                if first:
                    pe.wait_ge(wv_loaded, 16)
                for kind, n, c in start(attn, ffn):
                    if kind == "fill":
                        if first and n == 0:
                            pe.wait_ge(const_ready, CONSTS)
                        max_fill(j, 0, n)
                    elif kind == "row":
                        max_rows(j, 0)
                    else:
                        dense(j, (kind, n), c)
                if first:
                    pe.wait_ge(raw_summed, len(RAW))
                    mm(ps[:, MAX_BANK + 1, 0:len(RAW)], ones[:], absum[:], start=True, stop=True).then_inc(sums_ready, 1)
                    pe.wait_ge(thr_step, 3)
                    pe.wait_ge(wqk_loaded, 32)
                for t in range(QUADS):
                    pieces = placed(t, attn, ffn)
                    for pos in range(POS):
                        if attn and pos in FILL_AT:
                            fill(j, t, FILL_AT[pos])
                        if attn and pos in MAX_AT and t + 1 < QUADS:
                            max_fill(j, t + 1, MAX_AT[pos])
                        for u, c in pieces[pos]:
                            dense(j, u, c)
                        if attn and pos == ROW_AT and t + 1 < QUADS:
                            max_rows(j, t + 1)
                        if attn and pos == (SUM_AT if t + 1 < QUADS else LAST_SUM_AT):
                            weighted_sums(j, t)
                if first:
                    pe.wait_ge(wo_loaded, 16)
                    pe.wait_ge(ternary, len(RAW))

            pe.wait_ge(const_ready, FIRST_CONSTS)
            pe.wait_ge(wqk0_loaded, 32)
            dense_bank, order = banks(True, False), dense_order(True, False)
            iteration(0, True, False)
            dense_bank, order = banks(True, True), dense_order(True, True)
            with pe.Fori(1, B) as j:
                iteration(j, True, True)
            dense_bank, order = banks(False, True), dense_order(False, True)
            iteration(B, False, True)


def banks(attn, ffn):
    return {u: DENSE_BANK + n % 2 for n, u in enumerate(dense_order(attn, ffn))}


def max_bank(t, what, n):
    return MAX_BANK + (t * len(MAX_ORDER) + MAX_ORDER.index((what, n))) % 2


THR_STEPS = 8
FIRST_CONSTS = 4
CONSTS = 1 + 8 + 2 * (P // 32) + 1 + 2 * SLOTS + 1
_INS = ["x", "wq", "bq", "wk", "bk", "wv", "bv", "wo", "bo", "wg", "wu", "wd"]


def kernel(L0_attn_x, L0_attn_Wq, L0_attn_bq, L0_attn_Wk, L0_attn_bk, L0_attn_Wv, L0_attn_bv, L0_attn_Wo, L0_attn_bo,
           L0_ffn_w_gate, L0_ffn_w_up, L0_ffn_w_down):
    import numpy as np
    import concourse.bacc as bacc
    from concourse.bass_utils import run_bass_kernel_spmd

    def rows(w):
        w = np.asarray(w)
        r = w.reshape((BLOCKS, QH, 2, HD) + w.shape[1:])
        return np.ascontiguousarray(np.moveaxis(r, (2, 3, 1), (1, 2, 3)).reshape(w.shape))

    t = lambda w: np.ascontiguousarray(np.asarray(w).T)
    arrays = {
        "x": np.asarray(L0_attn_x), "wq": t(rows(L0_attn_Wq)), "bq": t(rows(L0_attn_bq).reshape(BLOCKS, P)), "wk": t(rows(L0_attn_Wk)),
        "bk": t(rows(L0_attn_bk).reshape(BLOCKS, P)), "wv": t(L0_attn_Wv), "bv": np.asarray(L0_attn_bv), "wo": t(L0_attn_Wo),
        "bo": np.asarray(L0_attn_bo), "wg": t(L0_ffn_w_gate), "wu": t(L0_ffn_w_up), "wd": t(L0_ffn_w_down),
    }
    nc = bacc.Bacc("TRN2", target_bir_lowering=False, num_devices=1)
    aps = [nc.dram_tensor(f"in_{n}", arrays[n].shape, mybir.dt.from_np(arrays[n].dtype), kind="ExternalInput").ap() for n in _INS]
    out = nc.dram_tensor("out", (B, L, D), F32, kind="ExternalOutput").ap()
    preln_block(nc, *aps, out)
    r = run_bass_kernel_spmd(nc, [{f"in_{n}": arrays[n] for n in _INS}], core_ids=[0])
    return r.results[0]["out"]
```
